# Optimizing a Trainium2 kernel written in Bass

```python
import numpy as np
import jax
import jax.numpy as jnp

def _softmax(x, axis=-1):
    return jax.nn.softmax(x, axis=axis)

def _gelu(x):
    return jax.nn.gelu(x, approximate=True)

def _silu(x):
    return jax.nn.silu(x)

def _sigmoid(x):
    return jax.nn.sigmoid(x)

def _layernorm(x, axis=-1, eps=1e-05):
    m = jnp.mean(x, axis=axis, keepdims=True)
    v = jnp.var(x, axis=axis, keepdims=True)
    return (x - m) / jnp.sqrt(v + eps)

def _scatter_add(tgt, idx, src, axis=0):
    return tgt.at[idx].add(src)

def _segment_sum(src, seg, n):
    return jax.ops.segment_sum(src, seg, n)
kernel_name = 'mk_dlrm_tower_d1_rec_r8_9054e4'

def setup_inputs(seed: int=0):
    np.random.seed(seed)
    _w = jnp.asarray

    def _rec_inputs():
        import jax
        import jax.numpy as jnp
        _tk = jax.random.key(seed)
        ids = jnp.stack([jax.random.randint(jax.random.fold_in(_tk, 200 + f), (2048,), 0, v, jnp.int32) for f, v in enumerate([125000, 1250, 1250, 1000, 1250, 12500, 1000, 12500, 1250, 1000, 1000, 1000, 1000, 1000, 1000, 1250, 12500, 1250, 1250, 12500, 12500, 1000, 1250, 1000, 1250, 12500])], axis=1)
        tbl_0 = 0.05 * jax.random.normal(jax.random.fold_in(_tk, 500 + 0), (125000, 128), jnp.float32)
        tbl_1 = 0.05 * jax.random.normal(jax.random.fold_in(_tk, 500 + 1), (1250, 128), jnp.float32)
        tbl_2 = 0.05 * jax.random.normal(jax.random.fold_in(_tk, 500 + 2), (1250, 128), jnp.float32)
        tbl_3 = 0.05 * jax.random.normal(jax.random.fold_in(_tk, 500 + 3), (1000, 128), jnp.float32)
        tbl_4 = 0.05 * jax.random.normal(jax.random.fold_in(_tk, 500 + 4), (1250, 128), jnp.float32)
        tbl_5 = 0.05 * jax.random.normal(jax.random.fold_in(_tk, 500 + 5), (12500, 128), jnp.float32)
        tbl_6 = 0.05 * jax.random.normal(jax.random.fold_in(_tk, 500 + 6), (1000, 128), jnp.float32)
        tbl_7 = 0.05 * jax.random.normal(jax.random.fold_in(_tk, 500 + 7), (12500, 128), jnp.float32)
        tbl_8 = 0.05 * jax.random.normal(jax.random.fold_in(_tk, 500 + 8), (1250, 128), jnp.float32)
        tbl_9 = 0.05 * jax.random.normal(jax.random.fold_in(_tk, 500 + 9), (1000, 128), jnp.float32)
        tbl_10 = 0.05 * jax.random.normal(jax.random.fold_in(_tk, 500 + 10), (1000, 128), jnp.float32)
        tbl_11 = 0.05 * jax.random.normal(jax.random.fold_in(_tk, 500 + 11), (1000, 128), jnp.float32)
        tbl_12 = 0.05 * jax.random.normal(jax.random.fold_in(_tk, 500 + 12), (1000, 128), jnp.float32)
        tbl_13 = 0.05 * jax.random.normal(jax.random.fold_in(_tk, 500 + 13), (1000, 128), jnp.float32)
        tbl_14 = 0.05 * jax.random.normal(jax.random.fold_in(_tk, 500 + 14), (1000, 128), jnp.float32)
        tbl_15 = 0.05 * jax.random.normal(jax.random.fold_in(_tk, 500 + 15), (1250, 128), jnp.float32)
        tbl_16 = 0.05 * jax.random.normal(jax.random.fold_in(_tk, 500 + 16), (12500, 128), jnp.float32)
        tbl_17 = 0.05 * jax.random.normal(jax.random.fold_in(_tk, 500 + 17), (1250, 128), jnp.float32)
        tbl_18 = 0.05 * jax.random.normal(jax.random.fold_in(_tk, 500 + 18), (1250, 128), jnp.float32)
        tbl_19 = 0.05 * jax.random.normal(jax.random.fold_in(_tk, 500 + 19), (12500, 128), jnp.float32)
        tbl_20 = 0.05 * jax.random.normal(jax.random.fold_in(_tk, 500 + 20), (12500, 128), jnp.float32)
        tbl_21 = 0.05 * jax.random.normal(jax.random.fold_in(_tk, 500 + 21), (1000, 128), jnp.float32)
        tbl_22 = 0.05 * jax.random.normal(jax.random.fold_in(_tk, 500 + 22), (1250, 128), jnp.float32)
        tbl_23 = 0.05 * jax.random.normal(jax.random.fold_in(_tk, 500 + 23), (1000, 128), jnp.float32)
        tbl_24 = 0.05 * jax.random.normal(jax.random.fold_in(_tk, 500 + 24), (1250, 128), jnp.float32)
        tbl_25 = 0.05 * jax.random.normal(jax.random.fold_in(_tk, 500 + 25), (12500, 128), jnp.float32)
        _rk = jax.random.fold_in(_tk, 7)
        r_bottom_output = -0.000520686 + 1.00062 * jax.random.normal(jax.random.fold_in(_rk, 101), (2048, 128), jnp.float32)
        W_top1 = 0.0456912 * jax.random.normal(jax.random.fold_in(_tk, 801), (479, 512), jnp.float32)
        W_top2 = 0.0441942 * jax.random.normal(jax.random.fold_in(_tk, 802), (512, 256), jnp.float32)
        W_top3 = 0.0625 * jax.random.normal(jax.random.fold_in(_tk, 803), (256, 1), jnp.float32)
        b_top1 = jnp.zeros((512,), jnp.float32)
        b_top2 = jnp.zeros((256,), jnp.float32)
        return (r_bottom_output, ids, tbl_0, tbl_1, tbl_2, tbl_3, tbl_4, tbl_5, tbl_6, tbl_7, tbl_8, tbl_9, tbl_10, tbl_11, tbl_12, tbl_13, tbl_14, tbl_15, tbl_16, tbl_17, tbl_18, tbl_19, tbl_20, tbl_21, tbl_22, tbl_23, tbl_24, tbl_25, W_top1, b_top1, W_top2, b_top2, W_top3)
    r_bottom_output, ids, tbl_0, tbl_1, tbl_2, tbl_3, tbl_4, tbl_5, tbl_6, tbl_7, tbl_8, tbl_9, tbl_10, tbl_11, tbl_12, tbl_13, tbl_14, tbl_15, tbl_16, tbl_17, tbl_18, tbl_19, tbl_20, tbl_21, tbl_22, tbl_23, tbl_24, tbl_25, W_top1, b_top1, W_top2, b_top2, W_top3 = _rec_inputs()

    def _L0_rec_setup():
        import jax, jax.numpy as jnp
        import numpy as np
        NUM_FEATURES = 27
        _TRIU_I, _TRIU_J = np.triu_indices(NUM_FEATURES, k=1)
        key = jax.random.key(seed)
        k1, k2 = jax.random.split(key)
        bottom_output = jax.random.normal(k1, (2048, 128), dtype=jnp.float32)
        embeddings = jax.random.normal(k2, (2048, 26, 128), dtype=jnp.float32)
        return {'bottom_output': bottom_output, 'embeddings': embeddings}
    _L0_rec_all = _L0_rec_setup()
    _L0_rec_in = {k: v for k, v in _L0_rec_all.items() if k in ()}
    del _L0_rec_all
    return {'r_bottom_output': r_bottom_output, 'ids': ids, 'tbl_0': tbl_0, 'tbl_1': tbl_1, 'tbl_2': tbl_2, 'tbl_3': tbl_3, 'tbl_4': tbl_4, 'tbl_5': tbl_5, 'tbl_6': tbl_6, 'tbl_7': tbl_7, 'tbl_8': tbl_8, 'tbl_9': tbl_9, 'tbl_10': tbl_10, 'tbl_11': tbl_11, 'tbl_12': tbl_12, 'tbl_13': tbl_13, 'tbl_14': tbl_14, 'tbl_15': tbl_15, 'tbl_16': tbl_16, 'tbl_17': tbl_17, 'tbl_18': tbl_18, 'tbl_19': tbl_19, 'tbl_20': tbl_20, 'tbl_21': tbl_21, 'tbl_22': tbl_22, 'tbl_23': tbl_23, 'tbl_24': tbl_24, 'tbl_25': tbl_25, 'W_top1': W_top1, 'b_top1': b_top1, 'W_top2': W_top2, 'b_top2': b_top2, 'W_top3': W_top3}

def reference(r_bottom_output, ids, tbl_0, tbl_1, tbl_2, tbl_3, tbl_4, tbl_5, tbl_6, tbl_7, tbl_8, tbl_9, tbl_10, tbl_11, tbl_12, tbl_13, tbl_14, tbl_15, tbl_16, tbl_17, tbl_18, tbl_19, tbl_20, tbl_21, tbl_22, tbl_23, tbl_24, tbl_25, W_top1, b_top1, W_top2, b_top2, W_top3):
    import jax
    import jax.numpy as jnp

    def _L0_rec_ref(bottom_output, embeddings):
        import jax, jax.numpy as jnp
        import numpy as np
        NUM_FEATURES = 27
        _TRIU_I, _TRIU_J = np.triu_indices(NUM_FEATURES, k=1)
        all_emb = jnp.concatenate([bottom_output[:, None, :], embeddings], axis=1)
        gram = jnp.einsum('bfd,bgd->bfg', all_emb, all_emb)
        return gram[:, _TRIU_I, _TRIU_J]
    e = jnp.stack([tbl_0[ids[:, 0]], tbl_1[ids[:, 1]], tbl_2[ids[:, 2]], tbl_3[ids[:, 3]], tbl_4[ids[:, 4]], tbl_5[ids[:, 5]], tbl_6[ids[:, 6]], tbl_7[ids[:, 7]], tbl_8[ids[:, 8]], tbl_9[ids[:, 9]], tbl_10[ids[:, 10]], tbl_11[ids[:, 11]], tbl_12[ids[:, 12]], tbl_13[ids[:, 13]], tbl_14[ids[:, 14]], tbl_15[ids[:, 15]], tbl_16[ids[:, 16]], tbl_17[ids[:, 17]], tbl_18[ids[:, 18]], tbl_19[ids[:, 19]], tbl_20[ids[:, 20]], tbl_21[ids[:, 21]], tbl_22[ids[:, 22]], tbl_23[ids[:, 23]], tbl_24[ids[:, 24]], tbl_25[ids[:, 25]]], axis=1)
    z = _L0_rec_ref(r_bottom_output, e)
    z = z.reshape(z.shape[0], -1)
    h = jnp.concatenate([z, r_bottom_output], axis=1)
    h = jnp.maximum(h @ W_top1 + b_top1, 0.0)
    h = jnp.maximum(h @ W_top2 + b_top2, 0.0)
    y = h @ W_top3
    return y

_drawn_inputs = setup_inputs


def setup_inputs(seed=0):
    import zlib

    import numpy as np

    out = dict(_drawn_inputs(seed))
    spreads = {'b_top1': (0.0, 0.1), 'b_top2': (0.0, 0.1)}
    factors = {}
    for name, (base, spread) in spreads.items():
        noise = np.random.default_rng([zlib.crc32(name.encode()), seed]).standard_normal(out[name].shape)
        drawn = base * np.exp(spread * noise) if base else spread * noise
        out[name] = jnp.asarray(drawn.astype(out[name].dtype))
    for name, factor in factors.items():
        out[name] = (out[name] * factor).astype(out[name].dtype)
    return out
```

```python
import numpy as np
import concourse.bass as bass
from concourse import mybir
from contextlib import ExitStack

P = 128
DIM = 128
TABLES = 26
BATCH = 2048
HALF = 128
BLOCK = 2 * HALF
BLOCKS = BATCH // BLOCK
TILES = BATCH // HALF
ONE_HOT_TABLES = [3, 6, 9, 10, 11]
GATHERED_TABLES = [t for t in range(TABLES) if t not in ONE_HOT_TABLES]
SLOT_FEATURE = [0] + [t + 1 for t in GATHERED_TABLES + ONE_HOT_TABLES]
FEATURES = len(SLOT_FEATURE)
SLOTS = 32
ROUNDS = 7
COLS = 4 * ROUNDS
PAIRS = FEATURES * (FEATURES - 1) // 2
N1, N2 = 512, 256


def tower(nc, x_d, ids_d, tables_d, w1_pairs_d, w1_x_d, b1_d, w2_d, b2_d, w3_d, y_d):
    f32, f32r, f16, i32 = (mybir.dt.float32, mybir.dt.float32r, mybir.dt.float16, mybir.dt.int32)
    ALU = mybir.AluOpType
    ACT = mybir.ActivationFunctionType

    GATHERED = len(GATHERED_TABLES)
    ONE_HOT = len(ONE_HOT_TABLES)
    VOCAB = tables_d[ONE_HOT_TABLES[0]].shape[0]
    CHUNKS = 8
    VP = VOCAB // CHUNKS
    HOT_BUFS = 3
    TURNED = 1 + GATHERED
    GROUPS = (TURNED + 3) // 4
    group_slots = [list(range(4 * g, min(4 * g + 4, TURNED))) for g in range(GROUPS)]
    K1 = N1 // P
    K2 = N2 // P
    SET = 32
    SETS = BLOCK // SET
    ID_BANKS = (ONE_HOT + 1) // 2

    uses, bank_uses = {}, [0, 0]

    def use(key, bank):
        uses[key] = (bank, bank_uses[bank])
        bank_uses[bank] += 1

    for h in range(2):
        for g in range(GROUPS):
            use(("turned", h, g), g % 2)
    for k in range(ONE_HOT):
        use(("hot", k), k % 2)

    ctx = ExitStack()
    with ctx:
        def sb(name, shape, dt):
            return ctx.enter_context(nc.sbuf_tensor(name, shape, dt))

        def pb(name, shape, dt=f32):
            return ctx.enter_context(nc.psum_tensor(name, shape, dt))

        def sem(name):
            return ctx.enter_context(nc.semaphore(name))

        ids_now = sb("ids_now", [P, 2, TABLES], i32)
        ids_all = sb("ids_all", [P, TILES, TABLES], i32)
        ids_hot = sb("ids_hot", [P, TILES, ONE_HOT], f16)
        rows = sb("rows", [P, 2, GATHERED, DIM], f32)
        x_rows = sb("x_rows", [P, 2, DIM], f32)
        feat = sb("feat", [P, BLOCK, SLOTS], f32)
        x_t = sb("x_t", [P, BLOCK], f32)
        pairs = sb("pairs", [P, ROUNDS, BLOCK], f32)
        table_raw = sb("table_raw", [VP, 2, CHUNKS * DIM], f32)
        table_hi = sb("table_hi", [VP, ONE_HOT, CHUNKS * DIM], f32r)
        table_lo = sb("table_lo", [VP, ONE_HOT, CHUNKS * DIM], f32r)
        row_ids_i = sb("row_ids_i", [P, CHUNKS], i32)
        row_ids = sb("row_ids", [P, CHUNKS], f32)
        ids_wide = sb("ids_wide", [VP, ONE_HOT, BLOCK], f32)
        hot = sb("hot", [VP, HOT_BUFS, CHUNKS, BLOCK], f32r)
        w1_pairs = sb("w1_pairs", [P, ROUNDS, N1], f32)
        w1_x = sb("w1_x", [P, N1], f32)
        w2 = sb("w2", [P, K1, N2], f32)
        w3 = sb("w3", [P, K2], f32)
        b1 = sb("b1", [P, K1], f32)
        b2 = sb("b2", [P, K2], f32)
        h1 = sb("h1", [P, K1, BLOCK], f32)
        h2 = sb("h2", [P, K2, BLOCK], f32)
        y_cols = sb("y_cols", [P, TILES], f32)
        y_rows = sb("y_rows", [TILES, P], f32)
        ident = sb("ident", [P, P], f32)
        ident16 = sb("ident16", [P, P], f16)

        feat_bank = [pb(f"feat_bank{n}", [P, 4, HALF]) for n in range(2)]
        gram_bank = [pb(f"gram_bank{n}", [P, 2, 512]) for n in range(2)]
        dense_bank = [pb(f"dense_bank{n}", [P, 2, BLOCK]) for n in range(2)]

        ids_all_in = sem("ids_all_in")
        ids_now_in = [sem(f"ids_now_in{h}") for h in range(2)]
        x_in = [sem(f"x_in{h}") for h in range(2)]
        gathered = [[sem(f"gathered{h}_{g}") for g in range(GROUPS)] for h in range(2)]
        weights_in = sem("weights_in")
        table_in = [sem(f"table_in{n}") for n in range(2)]
        table_hi_done = sem("table_hi_done")
        table_lo_done = sem("table_lo_done")
        passed = [sem("passed_pool"), sem("passed_sp")]
        pool_set = sem("pool_set")
        consts = sem("consts")
        iota_done = sem("iota_done")
        ident_done = sem("ident_done")
        feat_full = [sem(f"feat_full{n}") for n in range(2)]
        feat_out = [sem(f"feat_out{n}") for n in range(2)]
        wide_full = sem("wide_full")
        wide_out = sem("wide_out")
        hot_made = sem("hot_made")
        gram_full = sem("gram_full")
        pairs_act = sem("pairs_act")
        pairs_dve = sem("pairs_dve")
        x_t_done = sem("x_t_done")
        h1_full = sem("h1_full")
        h1_done = sem("h1_done")
        h2_full = sem("h2_full")
        h2_done = sem("h2_done")
        y_full = sem("y_full")
        y_done = sem("y_done")
        y_turned = sem("y_turned")
        y_ready = sem("y_ready")
        y_out = sem("y_out")

        block = ctx.enter_context(nc.Block())

        def ids_half(i, h):
            return ids_d.rearrange("(t p) f -> t p f", p=P)[bass.ds(2 * i + h, 1), :, :].rearrange("t p f -> (t p) f")

        def x_half(i, h):
            return x_d.rearrange("(t p) f -> t p f", p=P)[bass.ds(2 * i + h, 1), :, :].rearrange("t p f -> (t p) f")

        def wait_turned(eng, i, h, g):
            bank, before = uses[("turned", h, g)]
            eng.wait_ge(feat_full[bank], i * bank_uses[bank] + (before + 1))
            eng.sem_inc(passed[eng is nc.sync], 1)

        @block.sync
        def _(sp):
            for h in range(2):
                sp.dma_start(ids_now[:, h, :], ids_half(0, h)).then_inc(ids_now_in[h], 16)
            sp.dma_start(ids_all[:, :, :], ids_d.rearrange("(t p) f -> p t f", p=P)).then_inc(ids_all_in, 16)
            for h in range(2):
                sp.dma_start(x_rows[:, h, :], x_half(0, h)).then_inc(x_in[h], 16)
            for k, t in enumerate(ONE_HOT_TABLES):
                if k >= 2:
                    sp.wait_ge(table_lo_done, k - 1)
                sp.dma_start(table_raw[:, k % 2, :], tables_d[t].rearrange("(p c) d -> p (c d)", c=CHUNKS))\
                  .then_inc(table_in[k % 2], 16)
            sp.dma_start(w1_pairs[:, :, :], w1_pairs_d).then_inc(weights_in, 16)
            sp.dma_start(w1_x[:, :], w1_x_d).then_inc(weights_in, 16)
            sp.dma_start(w2[:, :, :], w2_d.rearrange("(k p) n -> p k n", p=P)).then_inc(weights_in, 16)
            sp.dma_start(b1[:, :], b1_d).then_inc(weights_in, 16)
            sp.dma_start(b2[:, :], b2_d).then_inc(weights_in, 16)
            sp.dma_start(w3[:, :], w3_d).then_inc(weights_in, 16)
            with sp.Fori(1, BLOCKS) as i:
                for h in range(2):
                    wait_turned(sp, i - 1, h, GROUPS - 2)
                    wait_turned(sp, i - 1, h, GROUPS - 1)
                    sp.dma_start(x_rows[:, h, :], x_half(i, h)).then_inc(x_in[h], 16)
                    sp.dma_start(ids_now[:, h, :], ids_half(i, h)).then_inc(ids_now_in[h], 16)
            sp.wait_ge(y_ready, 1)
            sp.dma_start(y_d.rearrange("(t p) o -> t (p o)", p=P), y_rows[:, :]).then_inc(y_out, 16)
            sp.wait_ge(y_out, 16)

        @block.gpsimd
        def _(pool):
            pool.memset(ident[:, :], 0.0).then_inc(pool_set, 1)
            pool.iota(row_ids_i[:, :], pattern=[[1, CHUNKS]], base=0, channel_multiplier=CHUNKS).then_inc(iota_done, 1)
            pool.wait_ge(pool_set, 1)
            pool.affine_select(out=ident[:, :], in_=ident[:, :], compare_op=ALU.not_equal, fill=1.0,
                               base=0, pattern=[[-1, P]], channel_multiplier=1).then_inc(ident_done, 1)

            def gathers(i, h, first):
                if not first:
                    pool.wait_ge(ids_now_in[h], 16 * (i + 1))
                    pool.sem_inc(passed[0], 1)
                else:
                    pool.wait_ge(ids_now_in[h], 16)
                for g, slots in enumerate(group_slots):
                    if not first:
                        wait_turned(pool, i - 1, h, g)
                    for s in slots:
                        if s == 0:
                            continue
                        t = GATHERED_TABLES[s - 1]
                        pool.indirect_dma_start(
                            out=rows[:, h, s - 1, :], out_offset=None, in_=tables_d[t],
                            in_offset=bass.IndirectOffsetOnAxis(ap=ids_now[:, h, t:t + 1], axis=0),
                        ).then_inc(gathered[h][g], 16)

            for h in range(2):
                gathers(0, h, True)
            with pool.Fori(1, BLOCKS) as i:
                for h in range(2):
                    gathers(i, h, False)

        def group_view(bank, n):
            return feat_bank[bank][:, 0:n, :].rearrange("p f b -> p b f")

        def gram_part(which, s, j):
            v = gram_bank[which][32 * s:32 * s + 32, :, 0:16 * COLS].rearrange(
                "p k (q u c) -> p k q u c", u=4, c=COLS)
            return v[:, :, :, s, ROUNDS * j:ROUNDS * (j + 1)]

        def pairs_part(n, s, j):
            v = pairs[32 * j:32 * j + 32, :, n * SET:(n + 1) * SET].rearrange(
                "p r (k q u) -> p k q u r", k=2, u=4)
            return v[:, :, :, s, :]

        @block.scalar
        def _(act):
            for k in range(ONE_HOT):
                act.wait_ge(table_in[k % 2], 16 * (k // 2 + 1))
                act.activation(table_hi[:, k, :], table_raw[:, k % 2, :], ACT.Copy).then_inc(table_hi_done, 1)
            act.wait_ge(weights_in, 6 * 16)

            def features_out(i, key, out, in_):
                bank, before = uses[key]
                act.wait_ge(feat_full[bank], i * bank_uses[bank] + (before + 1))
                act.activation(out, in_, ACT.Copy).then_inc(feat_out[bank], 1)

            def turned_out(i, h):
                for g, slots in enumerate(group_slots):
                    if g % 2 == 0:
                        features_out(i, ("turned", h, g), feat[:, h * HALF:(h + 1) * HALF, slots[0]:slots[-1] + 1],
                                     group_view(0, len(slots)))

            def dense(i):
                for c in range(K1):
                    act.wait_ge(h1_full, i * K1 + (c + 1))
                    act.activation(h1[:, c, :], dense_bank[c % 2][:, 0, :], ACT.Relu,
                                   bias=b1[:, c:c + 1]).then_inc(h1_done, 1)
                for c in range(K2):
                    act.wait_ge(h2_full, i * K2 + (c + 1))
                    act.activation(h2[:, c, :], dense_bank[c % 2][:, 0, :], ACT.Relu,
                                   bias=b2[:, c:c + 1]).then_inc(h2_done, 1)

            def out_column(i):
                act.wait_ge(y_full, i + 1)
                act.activation(y_cols[:, bass.ds(2 * i, 2)], dense_bank[0][:, 1, 0:2], ACT.Copy).then_inc(y_done, 1)

            def body(i, first):
                turned_out(i, 0)
                if not first:
                    dense(i - 1)
                turned_out(i, 1)
                if not first:
                    out_column(i - 1)
                for k in range(0, ONE_HOT, 2):
                    features_out(i, ("hot", k), feat[:, :, TURNED + k:TURNED + k + 1],
                                 feat_bank[0][:, 0:2, :].rearrange("p f b -> p (f b)").unsqueeze(2))
                for n in range(SETS):
                    act.wait_ge(gram_full, i * SETS + (n + 1))
                    for s in range(2):
                        for j in range(4):
                            last = act.activation(pairs_part(n, s, j), gram_part(n % 2, s, j), ACT.Copy)
                    last.then_inc(pairs_act, 1)

            body(0, True)
            with act.Fori(1, BLOCKS) as i:
                body(i, False)
            dense(BLOCKS - 1)
            out_column(BLOCKS - 1)

        @block.vector
        def _(dve):
            dve.memset(feat[:, :, FEATURES:SLOTS], 0.0).then_inc(consts, 1)
            dve.wait_ge(iota_done, 1)
            dve.tensor_copy(row_ids[:, :], row_ids_i[:, :]).then_inc(consts, 1)
            dve.wait_ge(ident_done, 1)
            dve.tensor_copy(ident16[:, :], ident[:, :]).then_inc(consts, 1)
            dve.wait_ge(ids_all_in, 16)
            for k, t in enumerate(ONE_HOT_TABLES):
                dve.tensor_copy(ids_hot[:, :, k:k + 1], ids_all[:, :, t:t + 1]).then_inc(consts, 1)
            dve.wait_ge(consts, 3 + ONE_HOT)

            def split_low(k):
                dve.wait_ge(table_hi_done, k + 1)
                dve.tensor_tensor(table_lo[:, k, :], table_raw[:, k % 2, :], table_hi[:, k, :].bitcast(f32),
                                  ALU.subtract).then_inc(table_lo_done, 1)

            def features_out(i, key, out, in_):
                bank, before = uses[key]
                dve.wait_ge(feat_full[bank], i * bank_uses[bank] + (before + 1))
                dve.tensor_copy(out, in_).then_inc(feat_out[bank], 1)

            def turned_out(i, h):
                for g, slots in enumerate(group_slots):
                    if g % 2 == 1:
                        features_out(i, ("turned", h, g), feat[:, h * HALF:(h + 1) * HALF, slots[0]:slots[-1] + 1],
                                     group_view(1, len(slots)))

            def ids_out(i, u):
                n = min(2, ONE_HOT - 2 * u)
                dve.wait_ge(wide_full, i * ID_BANKS + (u + 1))
                dve.tensor_copy(ids_wide[:, 2 * u:2 * u + n, :], dense_bank[u % 2][0:VP, 0:n, :]).then_inc(wide_out, 1)

            def make_hot(i, k, first):
                if k >= HOT_BUFS:
                    bank, before = uses[("hot", k - HOT_BUFS)]
                    dve.wait_ge(feat_full[bank], i * bank_uses[bank] + (before + 1))
                elif not first:
                    for last_k in (ONE_HOT - 2, ONE_HOT - 1):
                        bank, before = uses[("hot", last_k)]
                        dve.wait_ge(feat_full[bank], (i - 1) * bank_uses[bank] + (before + 1))
                for c in range(CHUNKS):
                    last = dve.tensor_scalar(hot[:, k % HOT_BUFS, c, :],
                                             ids_wide[:, k, :], row_ids[0:VP, c:c + 1], None, ALU.is_equal)
                last.then_inc(hot_made, 1)

            def body(i, first):
                for u in range(min(2, ID_BANKS)):
                    ids_out(i, u)
                turned_out(i, 0)
                for u in range(2, ID_BANKS):
                    ids_out(i, u)
                dve.wait_ge(wide_out, (i + 1) * ID_BANKS)
                for k in range(HOT_BUFS):
                    make_hot(i, k, first)
                turned_out(i, 1)
                for k in range(HOT_BUFS, ONE_HOT):
                    make_hot(i, k, first)
                for k in range(1, ONE_HOT, 2):
                    features_out(i, ("hot", k), feat[:, :, TURNED + k:TURNED + k + 1],
                                 feat_bank[1][:, 0:2, :].rearrange("p f b -> p (f b)").unsqueeze(2))
                bank, before = uses[("turned", 1, 0)]
                dve.wait_ge(feat_out[bank], i * bank_uses[bank] + (before + 1))
                if not first:
                    dve.wait_ge(h1_full, i * K1)
                dve.tensor_copy(x_t[:, :].unsqueeze(2), feat[:, :, 0:1]).then_inc(x_t_done, 1)
                for n in range(SETS):
                    dve.wait_ge(gram_full, i * SETS + (n + 1))
                    for s in range(2, 4):
                        for j in range(4):
                            last = dve.tensor_copy(pairs_part(n, s, j), gram_part(n % 2, s, j))
                    last.then_inc(pairs_dve, 1)

            for k in range(ONE_HOT):
                split_low(k)
            body(0, True)
            with dve.Fori(1, BLOCKS) as i:
                body(i, False)
            dve.wait_ge(y_turned, 1)
            dve.tensor_copy(y_rows[:, :], feat_bank[0][0:TILES, 0, :]).then_inc(y_ready, 1)

        @block.tensor
        def _(pe):
            def start_use(i, key, first):
                bank, before = uses[key]
                if not (first and before == 0):
                    pe.wait_ge(feat_out[bank], i * bank_uses[bank] + before)
                return bank

            def spread_ids(i, u):
                for n in range(min(2, ONE_HOT - 2 * u)):
                    k = 2 * u + n
                    for h in range(2):
                        mm = pe.matmul(dense_bank[u % 2][0:VP, n, h * HALF:(h + 1) * HALF],
                                       ids_hot[:, bass.ds(2 * i + h, 1), k:k + 1].rearrange("p t k -> p (t k)").to_broadcast([P, VP]),
                                       ident16[:, :], start=True, stop=True)
                mm.then_inc(wide_full, 1)

            def turn(i, h, first):
                for g, slots in enumerate(group_slots):
                    if g == 0:
                        pe.wait_ge(x_in[h], 16 * (i + 1))
                    pe.wait_ge(gathered[h][g], 16 * len([s for s in slots if s]) * (i + 1))
                    bank = start_use(i, ("turned", h, g), first)
                    for n, s in enumerate(slots):
                        src = x_rows[:, h, :] if s == 0 else rows[:, h, s - 1, :]
                        mm = pe.transpose(feat_bank[bank][:, n, :], src, ident[:, :])
                    mm.then_inc(feat_full[bank], 1)

            def one_hot(i, k, first):
                pe.wait_ge(hot_made, i * ONE_HOT + (k + 1))
                if first:
                    pe.wait_ge(table_lo_done, k + 1)
                bank = start_use(i, ("hot", k), first)
                out = feat_bank[bank][:, 0:2, :].rearrange("p f b -> p (f b)")
                n = 0
                for part in (table_hi, table_lo):
                    for c in range(CHUNKS):
                        mm = pe.matmul(out, part[:, k, c * DIM:(c + 1) * DIM], hot[:, k % HOT_BUFS, c, :],
                                       start=(n == 0), stop=(n == 2 * CHUNKS - 1))
                        n += 1
                mm.then_inc(feat_full[bank], 1)

            def products(i, n, first):
                if not (first and n < 2):
                    pe.wait_ge(pairs_act, i * SETS + (n - 1))
                    pe.wait_ge(pairs_dve, i * SETS + (n - 1))
                for q in range(SET // 4):
                    b = n * SET + 4 * q
                    mm = pe.matmul(gram_bank[n % 2][:, q // 4, (q % 4) * 4 * COLS:(q % 4 + 1) * 4 * COLS],
                                   feat[:, b:b + 4, :], feat[:, b:b + 4, 0:COLS], start=True, stop=True)
                mm.then_inc(gram_full, 1)

            def layer1(i, c):
                if c >= 2:
                    pe.wait_ge(h1_done, i * K1 + (c - 1))
                pe.matmul(dense_bank[c % 2][:, 0, :], w1_x[:, c * P:(c + 1) * P], x_t[:, :], start=True, stop=False)
                for r in range(ROUNDS):
                    mm = pe.matmul(dense_bank[c % 2][:, 0, :], w1_pairs[:, r, c * P:(c + 1) * P], pairs[:, r, :],
                                   start=False, stop=(r == ROUNDS - 1))
                mm.then_inc(h1_full, 1)

            def layer2(i, c):
                pe.wait_ge(h1_done, (i + 1) * K1)
                for k in range(K1):
                    mm = pe.matmul(dense_bank[c][:, 0, :], w2[:, k, c * P:(c + 1) * P], h1[:, k, :],
                                   start=(k == 0), stop=(k == K1 - 1))
                mm.then_inc(h2_full, 1)

            def layer3(i):
                pe.wait_ge(h2_done, (i + 1) * K2)
                for h in range(2):
                    for k in range(K2):
                        mm = pe.matmul(dense_bank[0][:, 1, h:h + 1], h2[:, k, h * HALF:(h + 1) * HALF], w3[:, k:k + 1],
                                       start=(k == 0), stop=(k == K2 - 1))
                mm.then_inc(y_full, 1)

            def dense(i):
                pe.wait_ge(x_t_done, i + 1)
                pe.wait_ge(pairs_act, (i + 1) * SETS)
                pe.wait_ge(pairs_dve, (i + 1) * SETS)
                for c in range(K1):
                    layer1(i, c)
                for c in range(K2):
                    layer2(i, c)

            def body(i, first):
                for u in range(min(2, ID_BANKS)):
                    spread_ids(i, u)
                turn(i, 0, first)
                for u in range(2, ID_BANKS):
                    pe.wait_ge(wide_out, i * ID_BANKS + (u - 1))
                    spread_ids(i, u)
                pe.wait_ge(wide_out, (i + 1) * ID_BANKS)
                if not first:
                    dense(i - 1)
                turn(i, 1, first)
                if not first:
                    layer3(i - 1)
                for k in range(ONE_HOT):
                    one_hot(i, k, first)
                for bank in range(2):
                    pe.wait_ge(feat_out[bank], (i + 1) * bank_uses[bank])
                for n in range(SETS):
                    products(i, n, first)
                if not first:
                    pe.wait_ge(y_done, i)

            pe.wait_ge(consts, 3 + ONE_HOT)
            pe.wait_ge(ident_done, 1)
            body(0, True)
            pe.wait_ge(weights_in, 6 * 16)
            with pe.Fori(1, BLOCKS) as i:
                body(i, False)
            dense(BLOCKS - 1)
            layer3(BLOCKS - 1)
            pe.wait_ge(y_done, BLOCKS)
            pe.transpose(feat_bank[0][0:TILES, 0, :], y_cols[:, :], ident[:, :]).then_inc(y_turned, 1)


def pair_row(f, g):
    return f * FEATURES - f * (f + 1) // 2 + (g - f - 1)


def paired_weights(w1):
    out = np.zeros((P, ROUNDS, N1), w1.dtype)
    for b in range(FEATURES):
        for a in range(b):
            f, g = sorted((SLOT_FEATURE[a], SLOT_FEATURE[b]))
            out[32 * (b // ROUNDS) + a, b % ROUNDS] = w1[pair_row(f, g)]
    return out


def kernel(**inputs):
    import concourse.bacc as bacc
    from concourse.bass_utils import run_bass_kernel_spmd

    w1 = np.asarray(inputs["W_top1"])
    arrays = {
        "in_x": np.asarray(inputs["r_bottom_output"]),
        "in_ids": np.asarray(inputs["ids"]),
        "in_w1_pairs": paired_weights(w1),
        "in_w1_x": np.ascontiguousarray(w1[PAIRS:]),
        "in_b1": np.ascontiguousarray(np.asarray(inputs["b_top1"]).reshape(N1 // P, P).T),
        "in_w2": np.asarray(inputs["W_top2"]),
        "in_b2": np.ascontiguousarray(np.asarray(inputs["b_top2"]).reshape(N2 // P, P).T),
        "in_w3": np.ascontiguousarray(np.asarray(inputs["W_top3"]).reshape(N2 // P, P).T),
    }
    for t in range(TABLES):
        arrays[f"in_tbl_{t}"] = np.asarray(inputs[f"tbl_{t}"])
    nc = bacc.Bacc("TRN2", target_bir_lowering=False, num_devices=1)
    d = {n: nc.dram_tensor(n, a.shape, mybir.dt.from_np(a.dtype), kind="ExternalInput").ap() for n, a in arrays.items()}
    y = nc.dram_tensor("out_y", (BATCH, 1), mybir.dt.float32, kind="ExternalOutput").ap()
    tower(nc, d["in_x"], d["in_ids"], [d[f"in_tbl_{t}"] for t in range(TABLES)], d["in_w1_pairs"], d["in_w1_x"],
          d["in_b1"], d["in_w2"], d["in_b2"], d["in_w3"], y)
    r = run_bass_kernel_spmd(nc, [arrays], core_ids=[0])
    return r.results[0]["out_y"]
```

```python
import numpy as np
import concourse.bass as bass
from concourse import mybir
from contextlib import ExitStack

P = 128
DIM = 128
TABLES = 26
BATCH = 2048
HALF = 128
BLOCK = 2 * HALF
BLOCKS = BATCH // BLOCK
TILES = BATCH // HALF
ONE_HOT_TABLES = [3, 6, 9, 10, 11, 12]
GATHERED_TABLES = [t for t in range(TABLES) if t not in ONE_HOT_TABLES]
SLOT_FEATURE = [0] + [t + 1 for t in GATHERED_TABLES + ONE_HOT_TABLES]
FEATURES = len(SLOT_FEATURE)
ROUNDS = 7
SLOTS = 4 * ROUNDS
QUAD = 32
PAIRS = FEATURES * (FEATURES - 1) // 2
N1, N2 = 512, 256
ONE_HOT = len(ONE_HOT_TABLES)
SPREADS = (ONE_HOT + 1) // 2
TURNED = 1 + len(GATHERED_TABLES)
GROUPS = (TURNED + 3) // 4
GROUP_SLOTS = [list(range(4 * g, min(4 * g + 4, TURNED))) for g in range(GROUPS)]
SET = 32
SETS = HALF // SET
W1_PARTS = (ROUNDS + 1) // 2
K1 = N1 // P
K2 = N2 // P
MASKS = ["upper", "minus_upper", "minus_lower"]
HOT_BUFS = 3
BEFORE, FIRST, STEADY, LAST = range(4)


def plan(which):
    spreads = [("spread", u) for u in range(SPREADS)]
    turns = [[("turn", h, g) for g in range(GROUPS)] for h in range(2)]
    next_makes = [("make", "next", k) for k in range(HOT_BUFS)]
    grams = [[("gram", h, n) for n in range(SETS)] + [("split", h)] for h in range(2)]
    layer1 = {m: [("layer1", m, c) for c in range(K1)] for m in ("prev", "own")}
    layer2 = {m: [("layer2", m, c) for c in range(K2)] for m in ("prev", "own")}
    tables = [("table", k) for k in range(ONE_HOT)]
    w1_parts = [("w1", k) for k in range(W1_PARTS)]
    lookups = [[("hot", k)] + [("make", "own", k + HOT_BUFS)] * (k + HOT_BUFS < ONE_HOT) for k in range(ONE_HOT)]

    def woven(*strands):
        return [step for n in range(max(map(len, strands))) for strand in strands for step in sum(strand[n:n + 1], [])]

    if which == BEFORE:
        return spreads + next_makes
    turned = [[[x] for x in turns[h]] for h in range(2)]
    if which == FIRST:
        out = tables[:2] + woven(turned[0], lookups, [[x] for x in tables[2:] + w1_parts[:2]]) + grams[0] + w1_parts[2:]
        out += woven(turned[1], [[x] for x in spreads], [[x] for x in next_makes])
        return out + grams[1]
    out = lookups[0] + lookups[1] + turns[0][:1] + lookups[2] + turns[0][1:2] + layer1["prev"][:1]
    out += woven(turned[0][2:5], lookups[3:], [[x] for x in layer1["prev"][1:3]] + [turns[0][5:] + layer1["prev"][3:]])
    if which == STEADY:
        out += spreads[:1] + grams[0][:1] + spreads[1:] + next_makes[:1] + turns[1][:1] + grams[0][1:2] + turns[1][1:2]
        out += layer2["prev"][:1] + next_makes[1:2] + turns[1][2:3] + grams[0][2:3] + turns[1][3:4]
        out += layer2["prev"][1:] + next_makes[2:] + turns[1][4:5] + grams[0][3:4] + turns[1][5:]
        return out + [("layer3", "prev")] + grams[0][4:] + grams[1]
    out += woven(turned[1][:5], [[x] for x in grams[0]]) + turns[1][5:] + layer2["prev"][:1] + grams[1]
    return out + layer2["prev"][1:] + [("layer3", "prev")] + layer1["own"] + layer2["own"] + [("layer3", "own")]


PLANS = [plan(which) for which in (BEFORE, FIRST, STEADY, LAST)]


def feature_uses(steps):
    return {step: n for n, step in enumerate(x for x in steps if x[0] in ("turn", "hot"))}


HOT_LAST = [max(k for k in range(ONE_HOT) if k % HOT_BUFS == n) for n in range(HOT_BUFS)]
USES = 2 * GROUPS + ONE_HOT


def tower(nc, x_d, ids_d, tables_d, w1_d, masks_d, b1_d, w2_d, b2_d, w3_d, y_d):
    f32, f32r, f16, i32 = (mybir.dt.float32, mybir.dt.float32r, mybir.dt.float16, mybir.dt.int32)
    ALU = mybir.AluOpType
    ACT = mybir.ActivationFunctionType

    VOCAB = tables_d[ONE_HOT_TABLES[0]].shape[0]
    CHUNKS = 8
    VP = VOCAB // CHUNKS
    ACT_SAMPLES = [3, 3]

    def number(i, m):
        return i - 1 if m == "prev" else i

    ctx = ExitStack()
    with ctx:
        def sb(name, shape, dt):
            return ctx.enter_context(nc.sbuf_tensor(name, shape, dt))

        def pb(name, shape, dt=f32):
            return ctx.enter_context(nc.psum_tensor(name, shape, dt))

        def sem(name):
            return ctx.enter_context(nc.semaphore(name))

        ids_now = sb("ids_now", [P, 2, TABLES], i32)
        ids_all = sb("ids_all", [P, TILES, TABLES], i32)
        ids_hot = sb("ids_hot", [P, TILES, ONE_HOT], f16)
        rows = sb("rows", [P, 2, len(GATHERED_TABLES), DIM], f32)
        x_rows = sb("x_rows", [P, 2, DIM], f32)
        feat = sb("feat", [P, 2, HALF, QUAD], f32)
        pairs = sb("pairs", [P, ROUNDS, BLOCK], f32)
        masks = sb("masks", [P, len(MASKS), ROUNDS + 1], f32)
        pairs_hi = sb("pairs_hi", [P, ROUNDS, BLOCK], f32r)
        pairs_mixed = sb("pairs_mixed", [P, ROUNDS, BLOCK], f32r)
        x_hi = sb("x_hi", [P, BLOCK], f32r)
        x_lo = sb("x_lo", [P, BLOCK], f32r)
        table_hi = sb("table_hi", [VP, ONE_HOT, CHUNKS * DIM], f32r)
        table_lo = sb("table_lo", [VP, ONE_HOT, CHUNKS * DIM], f32r)
        ids_wide = sb("ids_wide", [VP, ONE_HOT, BLOCK], f32)
        hot = sb("hot", [VP, HOT_BUFS, CHUNKS, BLOCK], f32r)
        row_ids_i = sb("row_ids_i", [P, CHUNKS], i32)
        row_ids = sb("row_ids", [P, CHUNKS], f32)
        ident = sb("ident", [P, P], f32)
        ident16 = sb("ident16", [P, P], f16)
        w1_upper = sb("w1_upper", [P, ROUNDS + 1, N1], f32r)
        w1_mixed = sb("w1_mixed", [P, ROUNDS + 1, N1], f32r)
        w2 = sb("w2", [P, K1, N2], f32)
        w3 = sb("w3", [P, K2], f32)
        b1 = sb("b1", [P, K1], f32)
        b2 = sb("b2", [P, K2], f32)
        h1 = sb("h1", [P, K1, BLOCK], f32)
        h2 = sb("h2", [P, K2, BLOCK], f32)
        raw = sb("raw", [P, CHUNKS * DIM], f32)
        y_cols = sb("y_cols", [P, TILES], f32)
        y_rows = sb("y_rows", [TILES, P], f32)

        feat_bank = [pb(f"feat_bank{n}", [P, 4, HALF]) for n in range(2)]
        gram_bank = [pb(f"gram_bank{n}", [P, 2, 512]) for n in range(2)]
        dense_bank = [pb(f"dense_bank{n}", [P, 2, BLOCK]) for n in range(2)]

        ids_now_in = [sem(f"ids_now_in{h}") for h in range(2)]
        ids_all_in = sem("ids_all_in")
        x_in = [sem(f"x_in{h}") for h in range(2)]
        staged_in = [sem(f"staged_in{n}") for n in range(3)]
        weights_in = sem("weights_in")
        iota_done = sem("iota_done")
        ident_cleared = sem("ident_cleared")
        ident_done = sem("ident_done")
        consts_done = sem("consts_done")
        pads_done = sem("pads_done")
        staged_hi = sem("staged_hi")
        staged_lo = sem("staged_lo")
        gathered = [[sem(f"gathered{h}_{g}") for g in range(GROUPS)] for h in range(2)]
        pool_passed = sem("pool_passed")
        sync_passed = sem("sync_passed")
        turned = sem("turned")
        looked_up = sem("looked_up")
        features_out = sem("features_out")
        spread = sem("spread")
        spread_out = sem("spread_out")
        hot_made = sem("hot_made")
        gram_done = sem("gram_done")
        pairs_act = sem("pairs_act")
        pairs_dve = sem("pairs_dve")
        x_hi_done = sem("x_hi_done")
        x_lo_done = sem("x_lo_done")
        pairs_hi_done = sem("pairs_hi_done")
        parts_done = sem("parts_done")
        h1_full = sem("h1_full")
        h1_done = sem("h1_done")
        h2_full = sem("h2_full")
        h2_done = sem("h2_done")
        y_full = sem("y_full")
        y_done = sem("y_done")
        y_turned = sem("y_turned")
        y_ready = sem("y_ready")
        y_out = sem("y_out")

        block = ctx.enter_context(nc.Block())

        def tile_of(dram, i, h):
            return dram.rearrange("(t p) f -> t p f", p=P)[bass.ds(2 * i + h, 1), :, :].rearrange("t p f -> (t p) f")

        def turns(i, h, g):
            return (2 * i + h) * GROUPS + (g + 1)

        def wait_features(engine, i, steps, h):
            last = max(n for x, n in feature_uses(steps).items() if x[0] == "hot" or x[:2] == ("turn", h))
            engine.wait_ge(features_out, i * USES + (last + 1))

        def feature_copy(step, bank):
            if step[0] == "turn":
                _, h, g = step
                s = GROUP_SLOTS[g]
                return feat[:, h, :, s[0]:s[-1] + 1], feat_bank[bank][:, 0:len(s), :].rearrange("p f b -> p b f")
            return feat[:, :, :, TURNED + step[1]], feat_bank[bank][:, 0:2, :]

        def gram_part(n, s, j):
            v = gram_bank[n % 2][32 * s:32 * s + 32, :, 0:16 * SLOTS].rearrange(
                "p k (q u c) -> p k q u c", u=4, c=SLOTS)
            return v[:, :, :, s, ROUNDS * j:ROUNDS * (j + 1)]

        def pairs_part(h, n, s, j):
            v = pairs[32 * j:32 * j + 32, 0:ROUNDS, h * HALF + n * SET:h * HALF + (n + 1) * SET].rearrange(
                "p r (k q u) -> p k q u r", k=2, u=4)
            return v[:, :, :, s, :]

        staging = [raw[:, :], h1[:, :, :].rearrange("p k b -> p (k b)"),
                   pairs[:, 0:CHUNKS * DIM // BLOCK, :].rearrange("p r b -> p (r b)")]
        STAGES = [n % 3 for n in range(ONE_HOT)] + [n % 2 for n in range(W1_PARTS)]

        def staged(step):
            kind, k = step
            if kind == "table":
                return k, staging[STAGES[k]][0:VP, :]
            n = ONE_HOT + k
            return n, staging[STAGES[n]].rearrange("p (r n) -> p r n", n=N1)

        def mask(name, r):
            return masks[:, MASKS.index(name), r:r + 1]

        @block.sync
        def _(sp):
            for h in range(2):
                sp.dma_start(ids_now[:, h, :], tile_of(ids_d, 0, h)).then_inc(ids_now_in[h], 16)
            sp.dma_start(ids_all[:, :, :], ids_d.rearrange("(t p) f -> p t f", p=P)).then_inc(ids_all_in, 16)

            def stage(n):
                before = [m for m in range(n) if STAGES[m] == STAGES[n]]
                if before:
                    sp.wait_ge(staged_lo, before[-1] + 1)
                if n < ONE_HOT:
                    src = tables_d[ONE_HOT_TABLES[n]].rearrange("(p c) d -> p (c d)", c=CHUNKS)
                    sp.dma_start(staging[STAGES[n]][0:VP, :], src).then_inc(staged_in[STAGES[n]], 16)
                else:
                    r = 2 * (n - ONE_HOT)
                    sp.dma_start(staging[STAGES[n]], w1_d[:, r:r + 2, :].rearrange("p r n -> p (r n)"))\
                      .then_inc(staged_in[STAGES[n]], 16)

            stage(0)
            for h in range(2):
                sp.dma_start(x_rows[:, h, :], tile_of(x_d, 0, h)).then_inc(x_in[h], 16)
            for n in range(1, 3):
                stage(n)
            sp.dma_start(masks[:, :, :], masks_d).then_inc(weights_in, 16)
            sp.dma_start(w2[:, :, :], w2_d.rearrange("(k p) n -> p k n", p=P)).then_inc(weights_in, 16)
            sp.dma_start(b1[:, :], b1_d).then_inc(weights_in, 16)
            sp.dma_start(b2[:, :], b2_d).then_inc(weights_in, 16)
            sp.dma_start(w3[:, :], w3_d).then_inc(weights_in, 16)
            for n in range(3, ONE_HOT + W1_PARTS):
                stage(n)
            with sp.Fori(1, BLOCKS) as i:
                for h in range(2):
                    for g in range(GROUPS):
                        sp.wait_ge(gathered[h][g], 16 * len([s for s in GROUP_SLOTS[g] if s]) * i)
                        sp.sem_inc(sync_passed, 1)
                    sp.dma_start(ids_now[:, h, :], tile_of(ids_d, i, h)).then_inc(ids_now_in[h], 16)
                    sp.wait_ge(turned, turns(i - 1, h, 0))
                    sp.sem_inc(sync_passed, 1)
                    sp.dma_start(x_rows[:, h, :], tile_of(x_d, i, h)).then_inc(x_in[h], 16)
            sp.wait_ge(y_ready, 1)
            sp.dma_start(y_d.rearrange("(t p) o -> t (p o)", p=P), y_rows[:, :]).then_inc(y_out, 16)
            sp.wait_ge(y_out, 16)

        @block.gpsimd
        def _(pool):
            pool.memset(ident[:, :], 0.0).then_inc(ident_cleared, 1)
            pool.iota(row_ids_i[:, :], pattern=[[1, CHUNKS]], base=0, channel_multiplier=CHUNKS).then_inc(iota_done, 1)
            pool.wait_ge(ident_cleared, 1)
            pool.affine_select(out=ident[:, :], in_=ident[:, :], compare_op=ALU.not_equal, fill=1.0,
                               base=0, pattern=[[-1, P]], channel_multiplier=1).then_inc(ident_done, 1)

            def gather(h, g):
                for s in GROUP_SLOTS[g]:
                    if s:
                        t = GATHERED_TABLES[s - 1]
                        pool.indirect_dma_start(
                            out=rows[:, h, s - 1, :], out_offset=None, in_=tables_d[t],
                            in_offset=bass.IndirectOffsetOnAxis(ap=ids_now[:, h, t:t + 1], axis=0),
                        ).then_inc(gathered[h][g], 16)

            for h in range(2):
                pool.wait_ge(ids_now_in[h], 16)
                for g in range(GROUPS):
                    gather(h, g)
            with pool.Fori(1, BLOCKS) as i:
                for h in range(2):
                    pool.wait_ge(ids_now_in[h], 16 * (i + 1))
                    pool.sem_inc(pool_passed, 1)
                    for g in range(GROUPS):
                        pool.wait_ge(turned, turns(i - 1, h, g))
                        pool.sem_inc(pool_passed, 1)
                        gather(h, g)

        @block.scalar
        def _(act):
            def walk(i, steps):
                uses = feature_uses(steps)
                for step in steps:
                    if step[0] in ("table", "w1"):
                        n, whole = staged(step)
                        act.wait_ge(staged_in[STAGES[n]], 16 * STAGES[:n + 1].count(STAGES[n]))
                        if step[0] == "table":
                            act.activation(table_hi[:, n, :], whole, ACT.Copy).then_inc(staged_hi, 1)
                        else:
                            for q in range(2):
                                r = 2 * step[1] + q
                                act.activation(w1_upper[:, r, :], whole[:, q, :], ACT.Identity, scale=mask("upper", r))
                                last = act.activation(w1_mixed[:, r, :], whole[:, q, :], ACT.Copy)
                            last.then_inc(staged_hi, 1)
                    elif step[0] == "spread":
                        u = step[1]
                        n = min(2, ONE_HOT - 2 * u)
                        act.wait_ge(spread, (i + 1) * SPREADS + (u + 1))
                        if steps is not PLANS[BEFORE]:
                            act.wait_ge(hot_made, i * ONE_HOT + (2 * u + n))
                        act.activation(ids_wide[:, 2 * u:2 * u + n, :], dense_bank[u % 2][0:VP, 0:n, :],
                                       ACT.Copy).then_inc(spread_out, 1)
                    elif step[0] in ("turn", "hot"):
                        if step[0] == "turn":
                            act.wait_ge(turned, turns(i, step[1], step[2]))
                        else:
                            act.wait_ge(looked_up, i * ONE_HOT + (step[1] + 1))
                        act.activation(*feature_copy(step, uses[step] % 2), ACT.Copy).then_inc(features_out, 1)
                    elif step[0] == "gram":
                        _, h, n = step
                        if n == 0:
                            wait_features(act, i, steps, h)
                            if steps is not PLANS[FIRST]:
                                act.wait_ge(h1_full, i * K1)
                            act.activation(x_hi[:, h * HALF:(h + 1) * HALF], feat[:, h, :, 0], ACT.Copy)\
                               .then_inc(x_hi_done, 1)
                            if steps is not PLANS[FIRST]:
                                act.wait_ge(parts_done, 2 * i + h - 1)
                        act.wait_ge(gram_done, (2 * i + h) * SETS + (n + 1))
                        for s, j in [(s, j) for s in range(ACT_SAMPLES[n % 2]) for j in range(4)]:
                            last = act.activation(pairs_part(h, n, s, j), gram_part(n, s, j), ACT.Copy)
                        last.then_inc(pairs_act, 1)
                    elif step[0] == "split":
                        h = step[1]
                        part = slice(h * HALF, (h + 1) * HALF)
                        act.wait_ge(pairs_act, (2 * i + h + 1) * SETS)
                        act.wait_ge(pairs_dve, (2 * i + h + 1) * SETS)
                        if steps is not PLANS[FIRST]:
                            act.wait_ge(h1_full, i * K1)
                        act.activation(pairs_hi[:, :, part], pairs[:, :, part], ACT.Copy).then_inc(pairs_hi_done, 1)
                    elif step[0] == "layer1":
                        _, m, c = step
                        act.wait_ge(h1_full, number(i, m) * K1 + (c + 1))
                        act.activation(h1[:, c, :], dense_bank[c % 2][:, 0, :], ACT.Relu,
                                       bias=b1[:, c:c + 1]).then_inc(h1_done, 1)
                    elif step[0] == "layer2":
                        _, m, c = step
                        act.wait_ge(h2_full, number(i, m) * K2 + (c + 1))
                        act.activation(h2[:, c, :], dense_bank[c][:, 0, :], ACT.Relu,
                                       bias=b2[:, c:c + 1]).then_inc(h2_done, 1)
                    elif step[0] == "layer3":
                        act.wait_ge(y_full, number(i, step[1]) + 1)
                        act.activation(y_cols[:, bass.ds(number(i, step[1]) * 2, 2)], dense_bank[0][:, 1, 0:2],
                                       ACT.Copy).then_inc(y_done, 1)

            walk(-1, PLANS[BEFORE])
            act.wait_ge(weights_in, 5 * 16)
            walk(0, PLANS[FIRST])
            with act.Fori(1, BLOCKS - 1) as i:
                walk(i, PLANS[STEADY])
            walk(BLOCKS - 1, PLANS[LAST])

        @block.vector
        def _(dve):
            dve.memset(feat[:, :, :, FEATURES:QUAD], 0.0).then_inc(pads_done, 1)
            dve.wait_ge(iota_done, 1)
            dve.tensor_copy(row_ids[:, :], row_ids_i[:, :]).then_inc(consts_done, 1)
            dve.wait_ge(ident_done, 1)
            dve.tensor_copy(ident16[:, :], ident[:, :]).then_inc(consts_done, 1)
            dve.wait_ge(ids_all_in, 16)
            for k, t in enumerate(ONE_HOT_TABLES):
                dve.tensor_copy(ids_hot[:, :, k:k + 1], ids_all[:, :, t:t + 1]).then_inc(consts_done, 1)
            dve.wait_ge(consts_done, 2 + ONE_HOT)

            def walk(i, steps):
                for step in steps:
                    if step[0] in ("table", "w1"):
                        n, whole = staged(step)
                        dve.wait_ge(staged_hi, n + 1)
                        if step[0] == "table":
                            last = dve.tensor_tensor(table_lo[:, n, :], whole, table_hi[:, n, :].bitcast(f32), ALU.subtract)
                        else:
                            for q in range(2):
                                r = 2 * step[1] + q
                                last = dve.scalar_tensor_tensor(
                                    out=w1_mixed[:, r, :], in0=w1_mixed[:, r, :].bitcast(f32),
                                    scalar=mask("minus_lower", r), in1=whole[:, q, :], op0=ALU.mult, op1=ALU.add)
                        last.then_inc(staged_lo, 1)
                    elif step[0] == "make":
                        _, m, k = step
                        made = i + 1 if m == "next" else i
                        dve.wait_ge(spread_out, made * SPREADS + (k // 2 + 1))
                        if m == "own":
                            dve.wait_ge(looked_up, i * ONE_HOT + (k - HOT_BUFS + 1))
                        elif steps is not PLANS[BEFORE]:
                            dve.wait_ge(looked_up, i * ONE_HOT + (HOT_LAST[k] + 1))
                        for c in range(CHUNKS):
                            last = dve.tensor_scalar(hot[:, k % HOT_BUFS, c, :], ids_wide[:, k, :],
                                                     row_ids[0:VP, c:c + 1], None, ALU.is_equal)
                        last.then_inc(hot_made, 1)
                    elif step[0] == "gram":
                        _, h, n = step
                        if n == 0:
                            dve.wait_ge(x_hi_done, 2 * i + h + 1)
                            dve.tensor_tensor(x_lo[:, h * HALF:(h + 1) * HALF], feat[:, h, :, 0],
                                              x_hi[:, h * HALF:(h + 1) * HALF].bitcast(f32), ALU.subtract)\
                               .then_inc(x_lo_done, 1)
                            if steps is not PLANS[FIRST]:
                                dve.wait_ge(parts_done, 2 * i + h - 1)
                        dve.wait_ge(gram_done, (2 * i + h) * SETS + (n + 1))
                        for s, j in [(s, j) for s in range(ACT_SAMPLES[n % 2], 4) for j in range(4)]:
                            last = dve.tensor_copy(pairs_part(h, n, s, j), gram_part(n, s, j))
                        last.then_inc(pairs_dve, 1)
                    elif step[0] == "split":
                        h = step[1]
                        part = slice(h * HALF, (h + 1) * HALF)
                        dve.wait_ge(pairs_hi_done, 2 * i + h + 1)
                        for r in range(ROUNDS):
                            last = dve.scalar_tensor_tensor(
                                out=pairs_mixed[:, r, part], in0=pairs_hi[:, r, part].bitcast(f32),
                                scalar=mask("minus_upper", r), in1=pairs[:, r, part], op0=ALU.mult, op1=ALU.add)
                        last.then_inc(parts_done, 1)

            walk(-1, PLANS[BEFORE])
            dve.wait_ge(weights_in, 5 * 16)
            walk(0, PLANS[FIRST])
            with dve.Fori(1, BLOCKS - 1) as i:
                walk(i, PLANS[STEADY])
            walk(BLOCKS - 1, PLANS[LAST])
            dve.wait_ge(y_turned, 1)
            dve.tensor_copy(y_rows[:, :], feat_bank[0][0:TILES, 0, :]).then_inc(y_ready, 1)

        @block.tensor
        def _(pe):
            def free_bank(i, steps, n):
                if n >= 2 or steps is not PLANS[FIRST]:
                    pe.wait_ge(features_out, i * USES + max(n - 1, 0))
                return n % 2

            def walk(i, steps):
                uses = feature_uses(steps)
                for step in steps:
                    if step[0] == "spread":
                        u = step[1]
                        if u >= 2:
                            pe.wait_ge(spread_out, (i + 1) * SPREADS + (u - 1))
                        elif steps is PLANS[STEADY]:
                            pe.wait_ge(h1_done, (i - 1) * K1 + (K1 - 1 + u))
                        for n in range(min(2, ONE_HOT - 2 * u)):
                            k = 2 * u + n
                            for h in range(2):
                                ids = ids_hot[:, bass.ds(2 * (i + 1) + h, 1), k:k + 1].rearrange("p t k -> p (t k)")
                                mm = pe.matmul(dense_bank[u % 2][0:VP, n, h * HALF:(h + 1) * HALF],
                                               ids.to_broadcast([P, VP]), ident16[:, :], start=True, stop=True)
                        mm.then_inc(spread, 1)
                    elif step[0] == "turn":
                        _, h, g = step
                        if g == 0:
                            pe.wait_ge(x_in[h], 16 * (i + 1))
                        pe.wait_ge(gathered[h][g], 16 * len([s for s in GROUP_SLOTS[g] if s]) * (i + 1))
                        bank = free_bank(i, steps, uses[step])
                        for n, s in enumerate(GROUP_SLOTS[g]):
                            src = rows[:, h, s - 1, :] if s else x_rows[:, h, :]
                            mm = pe.transpose(feat_bank[bank][:, n, :], src, ident[:, :])
                        mm.then_inc(turned, 1)
                    elif step[0] == "hot":
                        k = step[1]
                        if steps is PLANS[FIRST]:
                            pe.wait_ge(staged_lo, k + 1)
                        pe.wait_ge(hot_made, i * ONE_HOT + (k + 1))
                        bank = free_bank(i, steps, uses[step])
                        out = feat_bank[bank][:, 0:2, :].rearrange("p h b -> p (h b)")
                        for c in range(CHUNKS):
                            for part in (table_hi, table_lo):
                                mm = pe.matmul(out, part[:, k, c * DIM:(c + 1) * DIM], hot[:, k % HOT_BUFS, c, :],
                                               start=(c == 0 and part is table_hi),
                                               stop=(c == CHUNKS - 1 and part is table_lo))
                        mm.then_inc(looked_up, 1)
                    elif step[0] == "gram":
                        _, h, n = step
                        if n == 0:
                            wait_features(pe, i, steps, h)
                        if not (steps is PLANS[FIRST] and h == 0 and n < 2):
                            pe.wait_ge(pairs_act, (2 * i + h) * SETS + (n - 1))
                            pe.wait_ge(pairs_dve, (2 * i + h) * SETS + (n - 1))
                        for q in range(SET // 4):
                            b = n * SET + 4 * q
                            out = gram_bank[n % 2][:, q // 4, (q % 4) * 4 * SLOTS:(q % 4 + 1) * 4 * SLOTS]
                            mm = pe.matmul(out, feat[:, h, b:b + 4, :], feat[:, h, b:b + 4, 0:SLOTS], start=True, stop=True)
                        mm.then_inc(gram_done, 1)
                    elif step[0] == "layer1":
                        _, m, c = step
                        if c == 0:
                            pe.wait_ge(x_lo_done, 2 * (number(i, m) + 1))
                            pe.wait_ge(parts_done, 2 * (number(i, m) + 1))
                            pe.wait_ge(spread_out, (i + 1) * SPREADS)
                            pe.wait_ge(pairs_act, 2 * i * SETS)
                            if m == "own":
                                pe.wait_ge(y_done, i)
                        if c >= 2:
                            pe.wait_ge(h1_done, number(i, m) * K1 + (c - 1))
                        cols = slice(c * P, (c + 1) * P)
                        out = dense_bank[c % 2][:, 0, :]
                        for r in range(ROUNDS):
                            pe.matmul(out, w1_upper[:, r, cols], pairs_hi[:, r, :], start=(r == 0), stop=False)
                            pe.matmul(out, w1_mixed[:, r, cols], pairs_mixed[:, r, :], start=False, stop=False)
                        pe.matmul(out, w1_upper[:, ROUNDS, cols], x_hi[:, :], start=False, stop=False)
                        pe.matmul(out, w1_mixed[:, ROUNDS, cols], x_hi[:, :], start=False, stop=False)
                        mm = pe.matmul(out, w1_upper[:, ROUNDS, cols], x_lo[:, :], start=False, stop=True)
                        mm.then_inc(h1_full, 1)
                    elif step[0] == "layer2":
                        _, m, c = step
                        if c == 0 and steps is PLANS[STEADY]:
                            pe.wait_ge(spread_out, (i + 2) * SPREADS)
                        pe.wait_ge(h1_done, (number(i, m) + 1) * K1)
                        for k in range(K1):
                            mm = pe.matmul(dense_bank[c][:, 0, :], w2[:, k, c * P:(c + 1) * P], h1[:, k, :],
                                           start=(k == 0), stop=(k == K1 - 1))
                        mm.then_inc(h2_full, 1)
                    elif step[0] == "layer3":
                        m = number(i, step[1])
                        pe.wait_ge(h2_done, (m + 1) * K2)
                        for h in range(2):
                            for k in range(K2):
                                mm = pe.matmul(dense_bank[0][:, 1, h:h + 1], h2[:, k, h * HALF:(h + 1) * HALF],
                                               w3[:, k:k + 1], start=(k == 0), stop=(k == K2 - 1))
                        mm.then_inc(y_full, 1)

            pe.wait_ge(pads_done, 1)
            pe.wait_ge(consts_done, 2 + ONE_HOT)
            pe.wait_ge(ident_done, 1)
            walk(-1, PLANS[BEFORE])
            walk(0, PLANS[FIRST])
            pe.wait_ge(staged_lo, ONE_HOT + W1_PARTS)
            pe.wait_ge(weights_in, 5 * 16)
            with pe.Fori(1, BLOCKS - 1) as i:
                walk(i, PLANS[STEADY])
            walk(BLOCKS - 1, PLANS[LAST])
            pe.wait_ge(y_done, BLOCKS)
            pe.transpose(feat_bank[0][0:TILES, 0, :], y_cols[:, :], ident[:, :]).then_inc(y_turned, 1)


def pair_row(f, g):
    return f * FEATURES - f * (f + 1) // 2 + (g - f - 1)


def paired_weights(w1):
    out = np.zeros((P, ROUNDS + 1, N1), w1.dtype)
    out[:, ROUNDS] = w1[PAIRS:]
    for b in range(FEATURES):
        for a in (a for a in range(FEATURES) if a != b):
            f, g = sorted((SLOT_FEATURE[a], SLOT_FEATURE[b]))
            out[32 * (b // ROUNDS) + a, b % ROUNDS] = w1[pair_row(f, g)]
    return out


def places():
    place = np.arange(P)[:, None]
    slot_a, slot_b = place % QUAD, ROUNDS * (place // QUAD) + np.arange(ROUNDS)
    x = np.ones((P, 1))
    upper = np.concatenate([slot_a < slot_b, x], axis=1)
    lower = np.concatenate([slot_a > slot_b, x], axis=1)
    return np.stack([upper, -upper, -lower], axis=1).astype(np.float32)


def kernel(**inputs):
    import concourse.bacc as bacc
    from concourse.bass_utils import run_bass_kernel_spmd

    w1 = np.asarray(inputs["W_top1"])
    arrays = {
        "in_x": np.asarray(inputs["r_bottom_output"]),
        "in_ids": np.asarray(inputs["ids"]),
        "in_w1": paired_weights(w1),
        "in_masks": places(),
        "in_b1": np.ascontiguousarray(np.asarray(inputs["b_top1"]).reshape(N1 // P, P).T),
        "in_w2": np.asarray(inputs["W_top2"]),
        "in_b2": np.ascontiguousarray(np.asarray(inputs["b_top2"]).reshape(N2 // P, P).T),
        "in_w3": np.ascontiguousarray(np.asarray(inputs["W_top3"]).reshape(N2 // P, P).T),
    }
    for t in range(TABLES):
        arrays[f"in_tbl_{t}"] = np.asarray(inputs[f"tbl_{t}"])
    nc = bacc.Bacc("TRN2", target_bir_lowering=False, num_devices=1)
    d = {n: nc.dram_tensor(n, a.shape, mybir.dt.from_np(a.dtype), kind="ExternalInput").ap() for n, a in arrays.items()}
    y = nc.dram_tensor("out_y", (BATCH, 1), mybir.dt.float32, kind="ExternalOutput").ap()
    tower(nc, d["in_x"], d["in_ids"], [d[f"in_tbl_{t}"] for t in range(TABLES)], d["in_w1"], d["in_masks"],
          d["in_b1"], d["in_w2"], d["in_b2"], d["in_w3"], y)
    r = run_bass_kernel_spmd(nc, [arrays], core_ids=[0])
    return r.results[0]["out_y"]
```

```python
import numpy as np
import concourse.bass as bass
from concourse import mybir
from contextlib import ExitStack

P = 128
DIM = 128
TABLES = 26
BATCH = 2048
HALF = 128
BLOCK = 2 * HALF
BLOCKS = BATCH // BLOCK
TILES = BATCH // HALF
ONE_HOT_TABLES = [3, 6, 9, 10, 11, 12]
GATHERED_TABLES = [t for t in range(TABLES) if t not in ONE_HOT_TABLES]
SLOT_FEATURE = [0] + [t + 1 for t in GATHERED_TABLES + ONE_HOT_TABLES]
FEATURES = len(SLOT_FEATURE)
ROUNDS = 7
SLOTS = 4 * ROUNDS
QUAD = 32
PAIRS = FEATURES * (FEATURES - 1) // 2
N1, N2 = 512, 256
ONE_HOT = len(ONE_HOT_TABLES)
SPREADS = (ONE_HOT + 1) // 2
TURNED = 1 + len(GATHERED_TABLES)
GROUPS = (TURNED + 3) // 4
GROUP_SLOTS = [list(range(4 * g, min(4 * g + 4, TURNED))) for g in range(GROUPS)]
SET = 32
SETS = HALF // SET
W1_PARTS = (ROUNDS + 1) // 2
K1 = N1 // P
K2 = N2 // P
MASKS = ["upper", "minus_lower"]
HOT_BUFS = 2
BEFORE, FIRST, STEADY, LAST = range(4)


def plan(which):
    spreads = [("spread", u) for u in range(SPREADS)]
    turns = [[("turn", h, g) for g in range(GROUPS)] for h in range(2)]
    next_makes = [("make", "next", k) for k in range(HOT_BUFS)]
    grams = [[("gram", h, 0), ("gram", h, 1), ("gram", h, 2), ("split", h, 0), ("gram", h, 3), ("split", h, 1)]
             for h in range(2)]
    layer1 = {m: [("layer1", m, c) for c in range(K1)] for m in ("prev", "own")}
    layer2 = {m: [("layer2", m, c) for c in range(K2)] for m in ("prev", "own")}
    tables = [("table", k) for k in range(ONE_HOT)]
    w1_parts = [("w1", k) for k in range(W1_PARTS)]
    w2_part = [("w2", 0)]
    lookups = [[("hot", k)] + [("make", "own", k + HOT_BUFS)] * (k + HOT_BUFS < ONE_HOT) for k in range(ONE_HOT)]

    def woven(*strands):
        return [step for n in range(max(map(len, strands))) for strand in strands for step in sum(strand[n:n + 1], [])]

    if which == BEFORE:
        return spreads + next_makes[:1] + tables[:1] + next_makes[1:2] + tables[1:2] + next_makes[2:]
    turned = [[[x] for x in turns[h]] for h in range(2)]
    if which == FIRST:
        out = woven(lookups, turned[0], [[x] for x in tables[2:] + w1_parts[:1]]) + grams[0][:1] + spreads
        out += turns[1][:1] + grams[0][1:2] + w1_parts[1:2] + turns[1][1:2] + grams[0][2:3] + w1_parts[2:3]
        out += turns[1][2:3] + grams[0][3:] + next_makes[:1] + turns[1][3:4] + w1_parts[3:] + turns[1][4:] + w2_part
        return out + grams[1][:1] + next_makes[1:2] + grams[1][1:] + next_makes[2:]
    out = lookups[0] + lookups[1] + turns[0][:2]
    out += woven([[x] for x in layer1["prev"][:3]], lookups[2:5], turned[0][2:5])
    out += lookups[5] + turns[0][5:] + layer1["prev"][3:]
    if which == STEADY:
        out += spreads[:1] + grams[0][:1] + spreads[1:] + next_makes[:1] + turns[1][:1] + grams[0][1:2] + turns[1][1:2]
        out += layer2["prev"][:1] + next_makes[1:2] + turns[1][2:3] + grams[0][2:3] + turns[1][3:4]
        out += layer2["prev"][1:] + next_makes[2:] + turns[1][4:5] + grams[0][3:5] + turns[1][5:]
        return out + [("layer3", "prev")] + grams[0][5:] + grams[1]
    out += woven(turned[1][:4], [[x] for x in grams[0][:3]] + [grams[0][3:5]]) + layer2["prev"][:1] + turns[1][4:]
    out += grams[0][5:] + grams[1] + layer2["prev"][1:] + layer1["own"][:1] + [("layer3", "prev")]
    out += layer1["own"][1:] + layer2["own"]
    return out + [("layer3", "own")]


PLANS = [plan(which) for which in (BEFORE, FIRST, STEADY, LAST)]


def feature_uses(steps):
    return {step: n for n, step in enumerate(x for x in steps if x[0] in ("turn", "hot"))}


HOT_LAST = [max(k for k in range(ONE_HOT) if k % HOT_BUFS == n) for n in range(HOT_BUFS)]
USES = 2 * GROUPS + ONE_HOT


def tower(nc, x_d, ids_d, tables_d, w1_d, masks_d, b1_d, w2_d, b2_d, w3_d, y_d):
    f32, f32r, f16, i32 = (mybir.dt.float32, mybir.dt.float32r, mybir.dt.float16, mybir.dt.int32)
    ALU = mybir.AluOpType
    ACT = mybir.ActivationFunctionType

    VOCAB = tables_d[ONE_HOT_TABLES[0]].shape[0]
    CHUNKS = 8
    VP = VOCAB // CHUNKS
    ACT_SAMPLES = [3, 2]

    def number(i, m):
        return i - 1 if m == "prev" else i

    ctx = ExitStack()
    with ctx:
        def sb(name, shape, dt):
            return ctx.enter_context(nc.sbuf_tensor(name, shape, dt))

        def pb(name, shape, dt=f32):
            return ctx.enter_context(nc.psum_tensor(name, shape, dt))

        def sem(name):
            return ctx.enter_context(nc.semaphore(name))

        ids_now = sb("ids_now", [P, 2, TABLES], i32)
        ids_all = sb("ids_all", [P, TILES, TABLES], i32)
        ids_hot = sb("ids_hot", [P, TILES, ONE_HOT], f16)
        rows = sb("rows", [P, 2, len(GATHERED_TABLES), DIM], f32)
        x_rows = sb("x_rows", [P, 2, DIM], f32)
        feat = sb("feat", [P, 2, HALF, QUAD], f32)
        pairs = sb("pairs", [P, ROUNDS, BLOCK], f32)
        masks = sb("masks", [P, len(MASKS), ROUNDS + 1], f32)
        pairs_hi = sb("pairs_hi", [P, ROUNDS, BLOCK], f32r)
        pairs_lo = sb("pairs_lo", [P, ROUNDS, BLOCK], f32r)
        x_hi = sb("x_hi", [P, BLOCK], f32r)
        x_lo = sb("x_lo", [P, BLOCK], f32r)
        table_hi = sb("table_hi", [VP, ONE_HOT, CHUNKS * DIM], f32r)
        table_lo = sb("table_lo", [VP, ONE_HOT, CHUNKS * DIM], f32r)
        ids_wide = sb("ids_wide", [VP, ONE_HOT, BLOCK], f32)
        hot = sb("hot", [VP, HOT_BUFS, CHUNKS, BLOCK], f32r)
        row_ids_i = sb("row_ids_i", [P, CHUNKS], i32)
        row_ids = sb("row_ids", [P, CHUNKS], f32)
        ident = sb("ident", [P, P], f32)
        ident16 = sb("ident16", [P, P], f16)
        w1_upper = sb("w1_upper", [P, ROUNDS + 1, N1], f32r)
        w1_mixed = sb("w1_mixed", [P, ROUNDS + 1, N1], f32r)
        w2_hi = sb("w2_hi", [P, K1, N2], f32r)
        w2_lo = sb("w2_lo", [P, K1, N2], f32r)
        w3 = sb("w3", [P, K2], f32)
        b1 = sb("b1", [P, K1], f32)
        b2 = sb("b2", [P, K2], f32)
        h1 = sb("h1", [P, K1, BLOCK], f32)
        h1_hi = sb("h1_hi", [P, K1, BLOCK], f32r)
        h1_lo = sb("h1_lo", [P, K1, BLOCK], f32r)
        h2 = sb("h2", [P, K2, BLOCK], f32)
        raw = sb("raw", [P, CHUNKS * DIM], f32)
        y_cols = sb("y_cols", [P, TILES], f32)
        y_rows = sb("y_rows", [TILES, P], f32)

        feat_bank = [pb(f"feat_bank{n}", [P, 4, HALF]) for n in range(2)]
        gram_bank = [pb(f"gram_bank{n}", [P, 2, 512]) for n in range(2)]
        dense_bank = [pb(f"dense_bank{n}", [P, 2, BLOCK]) for n in range(2)]

        ids_now_in = [sem(f"ids_now_in{h}") for h in range(2)]
        ids_all_in = sem("ids_all_in")
        x_in = [sem(f"x_in{h}") for h in range(2)]
        staged_in = [sem(f"staged_in{n}") for n in range(3)]
        weights_in = sem("weights_in")
        iota_done = sem("iota_done")
        ident_cleared = sem("ident_cleared")
        ident_done = sem("ident_done")
        consts_done = sem("consts_done")
        pads_done = sem("pads_done")
        staged_hi = sem("staged_hi")
        staged_lo = sem("staged_lo")
        gathered = [[sem(f"gathered{h}_{g}") for g in range(GROUPS)] for h in range(2)]
        pool_passed = sem("pool_passed")
        sync_passed = sem("sync_passed")
        turned = sem("turned")
        looked_up = sem("looked_up")
        features_out = sem("features_out")
        spread = sem("spread")
        spread_out = sem("spread_out")
        hot_made = sem("hot_made")
        gram_done = sem("gram_done")
        pairs_act = sem("pairs_act")
        pairs_dve = sem("pairs_dve")
        x_hi_done = sem("x_hi_done")
        x_lo_done = sem("x_lo_done")
        pairs_hi_done = sem("pairs_hi_done")
        pairs_lo_done = sem("pairs_lo_done")
        h1_full = sem("h1_full")
        h1_done = sem("h1_done")
        h1_split = sem("h1_split")
        h2_full = sem("h2_full")
        h2_done = sem("h2_done")
        y_full = sem("y_full")
        y_done = sem("y_done")
        y_turned = sem("y_turned")
        y_ready = sem("y_ready")
        y_out = sem("y_out")

        block = ctx.enter_context(nc.Block())

        def tile_of(dram, i, h):
            return dram.rearrange("(t p) f -> t p f", p=P)[bass.ds(2 * i + h, 1), :, :].rearrange("t p f -> (t p) f")

        def turns(i, h, g):
            return (2 * i + h) * GROUPS + (g + 1)

        def wait_features(engine, i, steps, h):
            last = max(n for x, n in feature_uses(steps).items() if x[0] == "hot" or x[:2] == ("turn", h))
            engine.wait_ge(features_out, i * USES + (last + 1))

        def feature_copy(step, bank):
            if step[0] == "turn":
                _, h, g = step
                s = GROUP_SLOTS[g]
                return feat[:, h, :, s[0]:s[-1] + 1], feat_bank[bank][:, 0:len(s), :].rearrange("p f b -> p b f")
            return feat[:, :, :, TURNED + step[1]], feat_bank[bank][:, 0:2, :]

        def gram_part(n, s, j):
            v = gram_bank[n % 2][32 * s:32 * s + 32, :, 0:16 * SLOTS].rearrange(
                "p k (q u c) -> p k q u c", u=4, c=SLOTS)
            return v[:, :, :, s, ROUNDS * j:ROUNDS * (j + 1)]

        def pairs_part(h, n, s, j):
            v = pairs[32 * j:32 * j + 32, 0:ROUNDS, h * HALF + n * SET:h * HALF + (n + 1) * SET].rearrange(
                "p r (k q u) -> p k q u r", k=2, u=4)
            return v[:, :, :, s, :]

        staging = [raw[:, :], h1[:, :, :].rearrange("p k b -> p (k b)"),
                   pairs[:, 0:CHUNKS * DIM // BLOCK, :].rearrange("p r b -> p (r b)")]
        STAGES = [n % 3 for n in range(ONE_HOT)] + [n % 2 for n in range(W1_PARTS + 1)]

        def staged(step):
            kind, k = step
            if kind == "table":
                return k, staging[STAGES[k]][0:VP, :]
            if kind == "w1":
                return ONE_HOT + k, staging[STAGES[ONE_HOT + k]].rearrange("p (r n) -> p r n", n=N1)
            return ONE_HOT + W1_PARTS, staging[STAGES[-1]].rearrange("p (k n) -> p k n", n=N2)

        def mask(name, r):
            return masks[:, MASKS.index(name), r:r + 1]

        @block.sync
        def _(sp):
            for h in range(2):
                sp.dma_start(ids_now[:, h, :], tile_of(ids_d, 0, h)).then_inc(ids_now_in[h], 16)
            sp.dma_start(ids_all[:, :, :], ids_d.rearrange("(t p) f -> p t f", p=P)).then_inc(ids_all_in, 16)

            def stage(n):
                before = [m for m in range(n) if STAGES[m] == STAGES[n]]
                if before:
                    sp.wait_ge(staged_lo, before[-1] + 1)
                if n < ONE_HOT:
                    src = tables_d[ONE_HOT_TABLES[n]].rearrange("(p c) d -> p (c d)", c=CHUNKS)
                    sp.dma_start(staging[STAGES[n]][0:VP, :], src).then_inc(staged_in[STAGES[n]], 16)
                elif n == ONE_HOT + W1_PARTS:
                    sp.dma_start(staging[STAGES[n]].rearrange("p (k n) -> p k n", n=N2),
                                 w2_d.rearrange("(k p) n -> p k n", p=P)).then_inc(staged_in[STAGES[n]], 16)
                else:
                    r = 2 * (n - ONE_HOT)
                    sp.dma_start(staging[STAGES[n]], w1_d[:, r:r + 2, :].rearrange("p r n -> p (r n)"))\
                      .then_inc(staged_in[STAGES[n]], 16)

            stage(0)
            for h in range(2):
                sp.dma_start(x_rows[:, h, :], tile_of(x_d, 0, h)).then_inc(x_in[h], 16)
            for n in range(1, 3):
                stage(n)
            sp.dma_start(masks[:, :, :], masks_d).then_inc(weights_in, 16)
            sp.dma_start(b1[:, :], b1_d).then_inc(weights_in, 16)
            sp.dma_start(b2[:, :], b2_d).then_inc(weights_in, 16)
            sp.dma_start(w3[:, :], w3_d).then_inc(weights_in, 16)
            for n in range(3, len(STAGES)):
                stage(n)
            with sp.Fori(1, BLOCKS) as i:
                for h in range(2):
                    for g in range(GROUPS):
                        sp.wait_ge(gathered[h][g], 16 * len([s for s in GROUP_SLOTS[g] if s]) * i)
                        sp.sem_inc(sync_passed, 1)
                    sp.dma_start(ids_now[:, h, :], tile_of(ids_d, i, h)).then_inc(ids_now_in[h], 16)
                    sp.wait_ge(turned, turns(i - 1, h, 0))
                    sp.sem_inc(sync_passed, 1)
                    sp.dma_start(x_rows[:, h, :], tile_of(x_d, i, h)).then_inc(x_in[h], 16)
            sp.wait_ge(y_ready, 1)
            sp.dma_start(y_d.rearrange("(t p) o -> t (p o)", p=P), y_rows[:, :]).then_inc(y_out, 16)
            sp.wait_ge(y_out, 16)

        @block.gpsimd
        def _(pool):
            pool.memset(ident[:, :], 0.0).then_inc(ident_cleared, 1)
            pool.iota(row_ids_i[:, :], pattern=[[1, CHUNKS]], base=0, channel_multiplier=CHUNKS).then_inc(iota_done, 1)
            pool.wait_ge(ident_cleared, 1)
            pool.affine_select(out=ident[:, :], in_=ident[:, :], compare_op=ALU.not_equal, fill=1.0,
                               base=0, pattern=[[-1, P]], channel_multiplier=1).then_inc(ident_done, 1)

            def gather(h, g):
                for s in GROUP_SLOTS[g]:
                    if s:
                        t = GATHERED_TABLES[s - 1]
                        pool.indirect_dma_start(
                            out=rows[:, h, s - 1, :], out_offset=None, in_=tables_d[t],
                            in_offset=bass.IndirectOffsetOnAxis(ap=ids_now[:, h, t:t + 1], axis=0),
                        ).then_inc(gathered[h][g], 16)

            for h in range(2):
                pool.wait_ge(ids_now_in[h], 16)
                for g in range(GROUPS):
                    gather(h, g)
            with pool.Fori(1, BLOCKS) as i:
                for h in range(2):
                    pool.wait_ge(ids_now_in[h], 16 * (i + 1))
                    pool.sem_inc(pool_passed, 1)
                    for g in range(GROUPS):
                        pool.wait_ge(turned, turns(i - 1, h, g))
                        pool.sem_inc(pool_passed, 1)
                        gather(h, g)

        @block.scalar
        def _(act):
            def walk(i, steps):
                uses = feature_uses(steps)
                for step in steps:
                    if step[0] in ("table", "w1", "w2"):
                        n, whole = staged(step)
                        act.wait_ge(staged_in[STAGES[n]], 16 * STAGES[:n + 1].count(STAGES[n]))
                        if step[0] == "table":
                            act.activation(table_hi[:, n, :], whole, ACT.Copy).then_inc(staged_hi, 1)
                        elif step[0] == "w2":
                            act.activation(w2_hi[:, :, :], whole, ACT.Copy).then_inc(staged_hi, 1)
                        else:
                            r = 2 * step[1]
                            act.activation(w1_mixed[:, r:r + 2, :], whole, ACT.Copy).then_inc(staged_hi, 1)
                    elif step[0] == "spread":
                        u = step[1]
                        n = min(2, ONE_HOT - 2 * u)
                        act.wait_ge(spread, (i + 1) * SPREADS + (u + 1))
                        if steps is not PLANS[BEFORE]:
                            act.wait_ge(hot_made, i * ONE_HOT + (2 * u + n))
                        act.activation(ids_wide[:, 2 * u:2 * u + n, :], dense_bank[u % 2][0:VP, 0:n, :],
                                       ACT.Copy).then_inc(spread_out, 1)
                    elif step[0] in ("turn", "hot"):
                        if step[0] == "turn":
                            act.wait_ge(turned, turns(i, step[1], step[2]))
                        else:
                            act.wait_ge(looked_up, i * ONE_HOT + (step[1] + 1))
                        act.activation(*feature_copy(step, uses[step] % 2), ACT.Copy).then_inc(features_out, 1)
                    elif step[0] == "gram":
                        _, h, n = step
                        if n == 0:
                            wait_features(act, i, steps, h)
                            if steps is not PLANS[FIRST]:
                                act.wait_ge(h1_full, i * K1)
                            act.activation(x_hi[:, h * HALF:(h + 1) * HALF], feat[:, h, :, 0], ACT.Copy)\
                               .then_inc(x_hi_done, 1)
                            if steps is not PLANS[FIRST]:
                                act.wait_ge(pairs_lo_done, 2 * (2 * i + h - 1))
                        act.wait_ge(gram_done, (2 * i + h) * SETS + (n + 1))
                        for s, j in [(s, j) for s in range(ACT_SAMPLES[n % 2]) for j in range(4)]:
                            last = act.activation(pairs_part(h, n, s, j), gram_part(n, s, j), ACT.Copy)
                        last.then_inc(pairs_act, 1)
                    elif step[0] == "split":
                        _, h, q = step
                        part = slice(h * HALF + q * HALF // 2, h * HALF + (q + 1) * HALF // 2)
                        act.wait_ge(pairs_act, (2 * i + h) * SETS + 2 * (q + 1))
                        act.wait_ge(pairs_dve, (2 * i + h) * SETS + 2 * (q + 1))
                        if steps is not PLANS[FIRST]:
                            act.wait_ge(h1_full, i * K1)
                        act.activation(pairs_hi[:, :, part], pairs[:, :, part], ACT.Copy).then_inc(pairs_hi_done, 1)
                    elif step[0] == "layer1":
                        _, m, c = step
                        act.wait_ge(h1_full, number(i, m) * K1 + (c + 1))
                        act.activation(h1[:, c, :], dense_bank[c % 2][:, 0, :], ACT.Relu,
                                       bias=b1[:, c:c + 1]).then_inc(h1_done, 1)
                    elif step[0] == "layer2":
                        _, m, c = step
                        act.wait_ge(h2_full, number(i, m) * K2 + (c + 1))
                        act.activation(h2[:, c, :], dense_bank[c][:, 0, :], ACT.Relu,
                                       bias=b2[:, c:c + 1]).then_inc(h2_done, 1)
                    elif step[0] == "layer3":
                        act.wait_ge(y_full, number(i, step[1]) + 1)
                        act.activation(y_cols[:, bass.ds(number(i, step[1]) * 2, 2)], dense_bank[1][:, 1, 0:2],
                                       ACT.Copy).then_inc(y_done, 1)

            walk(-1, PLANS[BEFORE])
            walk(0, PLANS[FIRST])
            act.wait_ge(weights_in, 4 * 16)
            with act.Fori(1, BLOCKS - 1) as i:
                walk(i, PLANS[STEADY])
            walk(BLOCKS - 1, PLANS[LAST])

        @block.vector
        def _(dve):
            dve.memset(feat[:, :, :, FEATURES:QUAD], 0.0).then_inc(pads_done, 1)
            dve.wait_ge(iota_done, 1)
            dve.tensor_copy(row_ids[:, :], row_ids_i[:, :]).then_inc(consts_done, 1)
            dve.wait_ge(ident_done, 1)
            dve.tensor_copy(ident16[:, :], ident[:, :]).then_inc(consts_done, 1)
            dve.wait_ge(ids_all_in, 16)
            for k, t in enumerate(ONE_HOT_TABLES):
                dve.tensor_copy(ids_hot[:, :, k:k + 1], ids_all[:, :, t:t + 1]).then_inc(consts_done, 1)
            dve.wait_ge(consts_done, 2 + ONE_HOT)

            def walk(i, steps):
                for step in steps:
                    if step[0] in ("table", "w1", "w2"):
                        n, whole = staged(step)
                        dve.wait_ge(staged_hi, n + 1)
                        if step[0] == "table":
                            last = dve.tensor_tensor(table_lo[:, n, :], whole, table_hi[:, n, :].bitcast(f32), ALU.subtract)
                        elif step[0] == "w2":
                            last = dve.tensor_tensor(w2_lo[:, :, :], whole, w2_hi[:, :, :].bitcast(f32), ALU.subtract)
                        else:
                            dve.wait_ge(weights_in, 4 * 16)
                            for q in range(2):
                                r = 2 * step[1] + q
                                dve.tensor_scalar(w1_upper[:, r, :], w1_mixed[:, r, :].bitcast(f32), mask("upper", r), None,
                                                  ALU.mult)
                                last = dve.scalar_tensor_tensor(
                                    out=w1_mixed[:, r, :], in0=w1_mixed[:, r, :].bitcast(f32),
                                    scalar=mask("minus_lower", r), in1=whole[:, q, :], op0=ALU.mult, op1=ALU.add)
                        last.then_inc(staged_lo, 1)
                    elif step[0] == "layer1":
                        _, m, c = step
                        dve.wait_ge(h1_done, number(i, m) * K1 + (c + 1))
                        dve.tensor_copy(h1_hi[:, c, :], h1[:, c, :]).then_inc(h1_split, 1)
                        dve.wait_ge(h1_split, 2 * (number(i, m) * K1 + c) + 1)
                        dve.tensor_tensor(h1_lo[:, c, :], h1[:, c, :], h1_hi[:, c, :].bitcast(f32),
                                          ALU.subtract).then_inc(h1_split, 1)
                    elif step[0] == "make":
                        _, m, k = step
                        made = i + 1 if m == "next" else i
                        dve.wait_ge(spread_out, made * SPREADS + (k // 2 + 1))
                        if m == "own":
                            dve.wait_ge(looked_up, i * ONE_HOT + (k - HOT_BUFS + 1))
                        elif steps is not PLANS[BEFORE]:
                            dve.wait_ge(looked_up, i * ONE_HOT + (HOT_LAST[k] + 1))
                        for c in range(CHUNKS):
                            last = dve.tensor_scalar(hot[:, k % HOT_BUFS, c, :], ids_wide[:, k, :],
                                                     row_ids[0:VP, c:c + 1], None, ALU.is_equal)
                        last.then_inc(hot_made, 1)
                    elif step[0] == "gram":
                        _, h, n = step
                        if n == 0:
                            dve.wait_ge(x_hi_done, 2 * i + h + 1)
                            dve.tensor_tensor(x_lo[:, h * HALF:(h + 1) * HALF], feat[:, h, :, 0],
                                              x_hi[:, h * HALF:(h + 1) * HALF].bitcast(f32), ALU.subtract)\
                               .then_inc(x_lo_done, 1)
                            if steps is not PLANS[FIRST]:
                                dve.wait_ge(pairs_lo_done, 2 * (2 * i + h - 1))
                        dve.wait_ge(gram_done, (2 * i + h) * SETS + (n + 1))
                        for s, j in [(s, j) for s in range(ACT_SAMPLES[n % 2], 4) for j in range(4)]:
                            last = dve.tensor_copy(pairs_part(h, n, s, j), gram_part(n, s, j))
                        last.then_inc(pairs_dve, 1)
                    elif step[0] == "split":
                        _, h, q = step
                        part = slice(h * HALF + q * HALF // 2, h * HALF + (q + 1) * HALF // 2)
                        dve.wait_ge(pairs_hi_done, 2 * (2 * i + h) + q + 1)
                        dve.tensor_tensor(pairs_lo[:, :, part], pairs[:, :, part], pairs_hi[:, :, part].bitcast(f32),
                                          ALU.subtract).then_inc(pairs_lo_done, 1)

            walk(-1, PLANS[BEFORE])
            walk(0, PLANS[FIRST])
            with dve.Fori(1, BLOCKS - 1) as i:
                walk(i, PLANS[STEADY])
            walk(BLOCKS - 1, PLANS[LAST])
            dve.wait_ge(y_turned, 1)
            dve.tensor_copy(y_rows[:, :], feat_bank[0][0:TILES, 0, :]).then_inc(y_ready, 1)

        @block.tensor
        def _(pe):
            def free_bank(i, steps, n):
                if n >= 2 or steps is not PLANS[FIRST]:
                    pe.wait_ge(features_out, i * USES + max(n - 1, 0))
                return n % 2

            def walk(i, steps):
                uses = feature_uses(steps)
                for step in steps:
                    if step[0] == "spread":
                        u = step[1]
                        if u >= 2:
                            pe.wait_ge(spread_out, (i + 1) * SPREADS + (u - 1))
                        elif steps is PLANS[STEADY]:
                            pe.wait_ge(h1_done, (i - 1) * K1 + (K1 - 1 + u))
                        for n in range(min(2, ONE_HOT - 2 * u)):
                            k = 2 * u + n
                            for h in range(2):
                                ids = ids_hot[:, bass.ds(2 * (i + 1) + h, 1), k:k + 1].rearrange("p t k -> p (t k)")
                                mm = pe.matmul(dense_bank[u % 2][0:VP, n, h * HALF:(h + 1) * HALF],
                                               ids.to_broadcast([P, VP]), ident16[:, :], start=True, stop=True)
                        mm.then_inc(spread, 1)
                    elif step[0] == "turn":
                        _, h, g = step
                        if g == 0:
                            pe.wait_ge(x_in[h], 16 * (i + 1))
                        pe.wait_ge(gathered[h][g], 16 * len([s for s in GROUP_SLOTS[g] if s]) * (i + 1))
                        bank = free_bank(i, steps, uses[step])
                        for n, s in enumerate(GROUP_SLOTS[g]):
                            src = rows[:, h, s - 1, :] if s else x_rows[:, h, :]
                            mm = pe.transpose(feat_bank[bank][:, n, :], src, ident[:, :])
                        mm.then_inc(turned, 1)
                    elif step[0] == "hot":
                        k = step[1]
                        if steps is PLANS[FIRST]:
                            pe.wait_ge(staged_lo, k + 1)
                        pe.wait_ge(hot_made, i * ONE_HOT + (k + 1))
                        bank = free_bank(i, steps, uses[step])
                        out = feat_bank[bank][:, 0:2, :].rearrange("p h b -> p (h b)")
                        for c in range(CHUNKS):
                            for part in (table_hi, table_lo):
                                mm = pe.matmul(out, part[:, k, c * DIM:(c + 1) * DIM], hot[:, k % HOT_BUFS, c, :],
                                               start=(c == 0 and part is table_hi),
                                               stop=(c == CHUNKS - 1 and part is table_lo))
                        mm.then_inc(looked_up, 1)
                    elif step[0] == "gram":
                        _, h, n = step
                        if n == 0:
                            wait_features(pe, i, steps, h)
                        if not (steps is PLANS[FIRST] and h == 0 and n < 2):
                            pe.wait_ge(pairs_act, (2 * i + h) * SETS + (n - 1))
                            pe.wait_ge(pairs_dve, (2 * i + h) * SETS + (n - 1))
                        for q in range(SET // 4):
                            b = n * SET + 4 * q
                            out = gram_bank[n % 2][:, q // 4, (q % 4) * 4 * SLOTS:(q % 4 + 1) * 4 * SLOTS]
                            mm = pe.matmul(out, feat[:, h, b:b + 4, :], feat[:, h, b:b + 4, 0:SLOTS], start=True, stop=True)
                        mm.then_inc(gram_done, 1)
                    elif step[0] == "layer1":
                        _, m, c = step
                        if c == 0:
                            pe.wait_ge(x_lo_done, 2 * (number(i, m) + 1))
                            pe.wait_ge(spread_out, (i + 1) * SPREADS)
                            pe.wait_ge(pairs_act, 2 * i * SETS)
                            if m == "own":
                                pe.wait_ge(h2_done, i * K2 - 1)
                        elif c == 1 and m == "own":
                            pe.wait_ge(y_done, i)
                        if c >= 2:
                            pe.wait_ge(h1_done, number(i, m) * K1 + (c - 1))
                        cols = slice(c * P, (c + 1) * P)
                        out = dense_bank[c % 2][:, 0, :]
                        pe.matmul(out, w1_upper[:, ROUNDS, cols], x_hi[:, :], start=True, stop=False)
                        pe.matmul(out, w1_mixed[:, ROUNDS, cols], x_hi[:, :], start=False, stop=False)
                        pe.matmul(out, w1_upper[:, ROUNDS, cols], x_lo[:, :], start=False, stop=False)
                        if c == 0:
                            pe.wait_ge(pairs_hi_done, 4 * (number(i, m) + 1))
                        for r in range(ROUNDS):
                            pe.matmul(out, w1_mixed[:, r, cols], pairs_hi[:, r, :], start=False, stop=False)
                        if c == 0:
                            pe.wait_ge(pairs_lo_done, 4 * (number(i, m) + 1))
                        for r in range(ROUNDS):
                            mm = pe.matmul(out, w1_upper[:, r, cols], pairs_lo[:, r, :], start=False,
                                           stop=(r == ROUNDS - 1))
                        mm.then_inc(h1_full, 1)
                    elif step[0] == "layer2":
                        _, m, c = step
                        if c == 0 and steps is PLANS[STEADY]:
                            pe.wait_ge(spread_out, (i + 2) * SPREADS)
                        pe.wait_ge(h1_done, number(i, m) * K1 + (K1 - 1 + c))
                        out = dense_bank[c][:, 0, :]
                        cols = slice(c * P, (c + 1) * P)
                        for k in range(K1):
                            pe.wait_ge(h1_split, 2 * (number(i, m) * K1 + k) + 1)
                            pe.matmul(out, w2_hi[:, k, cols], h1_hi[:, k, :], start=(k == 0), stop=False)
                            pe.matmul(out, w2_lo[:, k, cols], h1_hi[:, k, :], start=False, stop=False)
                            pe.wait_ge(h1_split, 2 * (number(i, m) * K1 + (k + 1)))
                            mm = pe.matmul(out, w2_hi[:, k, cols], h1_lo[:, k, :], start=False, stop=(k == K1 - 1))
                        mm.then_inc(h2_full, 1)
                    elif step[0] == "layer3":
                        m = number(i, step[1])
                        pe.wait_ge(h2_done, (m + 1) * K2)
                        for h in range(2):
                            for k in range(K2):
                                mm = pe.matmul(dense_bank[1][:, 1, h:h + 1], h2[:, k, h * HALF:(h + 1) * HALF],
                                               w3[:, k:k + 1], start=(k == 0), stop=(k == K2 - 1))
                        mm.then_inc(y_full, 1)

            pe.wait_ge(pads_done, 1)
            pe.wait_ge(consts_done, 2 + ONE_HOT)
            pe.wait_ge(ident_done, 1)
            walk(-1, PLANS[BEFORE])
            walk(0, PLANS[FIRST])
            pe.wait_ge(staged_lo, len(STAGES))
            pe.wait_ge(weights_in, 4 * 16)
            with pe.Fori(1, BLOCKS - 1) as i:
                walk(i, PLANS[STEADY])
            walk(BLOCKS - 1, PLANS[LAST])
            pe.wait_ge(y_done, BLOCKS)
            pe.transpose(feat_bank[0][0:TILES, 0, :], y_cols[:, :], ident[:, :]).then_inc(y_turned, 1)


def pair_row(f, g):
    return f * FEATURES - f * (f + 1) // 2 + (g - f - 1)


def paired_weights(w1):
    out = np.zeros((P, ROUNDS + 1, N1), w1.dtype)
    out[:, ROUNDS] = w1[PAIRS:]
    for b in range(FEATURES):
        for a in (a for a in range(FEATURES) if a != b):
            f, g = sorted((SLOT_FEATURE[a], SLOT_FEATURE[b]))
            out[32 * (b // ROUNDS) + a, b % ROUNDS] = w1[pair_row(f, g)]
    return out


def places():
    place = np.arange(P)[:, None]
    slot_a, slot_b = place % QUAD, ROUNDS * (place // QUAD) + np.arange(ROUNDS)
    x = np.ones((P, 1))
    upper = np.concatenate([slot_a < slot_b, x], axis=1)
    lower = np.concatenate([slot_a > slot_b, x], axis=1)
    return np.stack([upper, -lower], axis=1).astype(np.float32)


def kernel(**inputs):
    import concourse.bacc as bacc
    from concourse.bass_utils import run_bass_kernel_spmd

    w1 = np.asarray(inputs["W_top1"])
    arrays = {
        "in_x": np.asarray(inputs["r_bottom_output"]),
        "in_ids": np.asarray(inputs["ids"]),
        "in_w1": paired_weights(w1),
        "in_masks": places(),
        "in_b1": np.ascontiguousarray(np.asarray(inputs["b_top1"]).reshape(N1 // P, P).T),
        "in_w2": np.asarray(inputs["W_top2"]),
        "in_b2": np.ascontiguousarray(np.asarray(inputs["b_top2"]).reshape(N2 // P, P).T),
        "in_w3": np.ascontiguousarray(np.asarray(inputs["W_top3"]).reshape(N2 // P, P).T),
    }
    for t in range(TABLES):
        arrays[f"in_tbl_{t}"] = np.asarray(inputs[f"tbl_{t}"])
    nc = bacc.Bacc("TRN2", target_bir_lowering=False, num_devices=1)
    d = {n: nc.dram_tensor(n, a.shape, mybir.dt.from_np(a.dtype), kind="ExternalInput").ap() for n, a in arrays.items()}
    y = nc.dram_tensor("out_y", (BATCH, 1), mybir.dt.float32, kind="ExternalOutput").ap()
    tower(nc, d["in_x"], d["in_ids"], [d[f"in_tbl_{t}"] for t in range(TABLES)], d["in_w1"], d["in_masks"],
          d["in_b1"], d["in_w2"], d["in_b2"], d["in_w3"], y)
    r = run_bass_kernel_spmd(nc, [arrays], core_ids=[0])
    return r.results[0]["out_y"]
```
